# Optimizing a Trainium2 kernel written in Bass

```python
import numpy as np
import jax
import jax.numpy as jnp

def _softmax(x, axis=-1):
    return jax.nn.softmax(x, axis=axis)
def _gelu(x):
    return jax.nn.gelu(x, approximate=True)
def _silu(x):
    return jax.nn.silu(x)
def _sigmoid(x):
    return jax.nn.sigmoid(x)
def _layernorm(x, axis=-1, eps=1e-5):
    m = jnp.mean(x, axis=axis, keepdims=True)
    v = jnp.var(x, axis=axis, keepdims=True)
    return (x - m) / jnp.sqrt(v + eps)
def _scatter_add(tgt, idx, src, axis=0):
    return tgt.at[idx].add(src)
def _segment_sum(src, seg, n):
    return jax.ops.segment_sum(src, seg, n)

kernel_name = 'mk_adj_seq_d2_adj_256_26611e'

def setup_inputs(seed: int = 0):
    np.random.seed(seed)
    _w = jnp.asarray
    def _rec_inputs():
        import jax
        import jax.numpy as jnp
        _gk = jax.random.key(seed)
        x = -0.0005207 + 1.001 * jax.random.normal(jax.random.fold_in(_gk, 1), (64, 256, 256), jnp.float32)
        _a = jax.random.bernoulli(jax.random.fold_in(_gk, 2), 0.03125, (64, 256, 256))
        _a = jnp.logical_or(_a, jnp.swapaxes(_a, -1, -2))
        _a = jnp.logical_or(_a, jnp.eye(256, dtype=bool))
        adj = _a.astype(jnp.int32)
        return x, adj
    x, adj = _rec_inputs()
    def _L0_gnn_setup():
        import jax, jax.numpy as jnp
        import numpy as np
        ALPHA = 0.2
        NEG = -9000000000000000.0
        EPS = 1e-05

        def _gat(h, adj, W, a, out_features):
            Wh = jnp.matmul(h, W)
            Wh1 = jnp.matmul(Wh, a[:out_features])
            Wh2 = jnp.matmul(Wh, a[out_features:])
            e = Wh1 + jnp.swapaxes(Wh2, 1, 2)
            e = jax.nn.leaky_relu(e, negative_slope=ALPHA)
            scores = jnp.where(adj > 0, e, NEG)
            att = jax.nn.softmax(scores, axis=1)
            return jnp.matmul(att, Wh)

        def _layernorm(x, g, b):
            mu = jnp.mean(x, axis=-1, keepdims=True)
            var = jnp.var(x, axis=-1, keepdims=True)
            return (x - mu) * jax.lax.rsqrt(var + EPS) * g + b
        key = jax.random.key(seed)
        ks = jax.random.split(key, 8)
        B, N, F, H = (2, 4096, 256, 1024)
        x = jax.random.normal(ks[0], (B, N, F), dtype=jnp.float32)
        adj = jax.random.randint(ks[1], (B, N, N), 0, 2, dtype=jnp.int32)

        def xavier(k, shape):
            fan_in, fan_out = (shape[0], shape[1])
            lim = np.sqrt(6.0 / (fan_in + fan_out))
            return jax.random.uniform(k, shape, jnp.float32, -lim, lim)
        return {'x': x, 'adj': adj, 'W1': xavier(ks[2], (F, F)), 'a1': xavier(ks[3], (2 * F, 1)), 'W2': xavier(ks[4], (F, F)), 'a2': xavier(ks[5], (2 * F, 1)), 'w_ff1': xavier(ks[6], (F, H)), 'b_ff1': jnp.zeros((H,), jnp.float32), 'w_ff2': xavier(ks[7], (H, F)), 'b_ff2': jnp.zeros((F,), jnp.float32), 'g_ln1': jnp.ones((F,), jnp.float32), 'b_ln1': jnp.zeros((F,), jnp.float32), 'g_ln2': jnp.ones((F,), jnp.float32), 'b_ln2': jnp.zeros((F,), jnp.float32)}
    _L0_gnn_all = _L0_gnn_setup()
    _L0_gnn_in = {k: v for k, v in _L0_gnn_all.items() if k in ('W1', 'a1', 'W2', 'a2', 'w_ff1', 'b_ff1', 'w_ff2', 'b_ff2', 'g_ln1', 'b_ln1', 'g_ln2', 'b_ln2', )}
    del _L0_gnn_all

    def _L1_gnn_setup():
        import jax, jax.numpy as jnp
        import numpy as np
        B, N, D = (8, 1024, 256)
        H = 8
        DH = D // H
        R = 4
        FF = 1024
        EPS = 1e-05

        def _lin(k, fan_in, shape):
            return jax.random.normal(k, shape, jnp.float32) * (1.0 / np.sqrt(fan_in))

        def _ln(x, g, b):
            m = x.mean(-1, keepdims=True)
            v = ((x - m) ** 2).mean(-1, keepdims=True)
            return (x - m) * jax.lax.rsqrt(v + EPS) * g + b
        key = jax.random.key(seed)
        ks = jax.random.split(key, 16)
        src = jax.random.normal(ks[0], (B, N, D), jnp.float32)
        adj_matrix = jax.random.randint(ks[1], (B, N, N), 0, 5, dtype=jnp.int32)
        Wq = _lin(ks[2], D, (D, D))
        bq = jnp.zeros((D,), jnp.float32)
        Wk = _lin(ks[3], D, (D, D))
        bk = jnp.zeros((D,), jnp.float32)
        Wv = _lin(ks[4], D, (R, D, D))
        bv = jnp.zeros((R, D), jnp.float32)
        Wo = _lin(ks[5], D, (D, D))
        bo = jnp.zeros((D,), jnp.float32)
        W1 = _lin(ks[6], D, (D, FF))
        b1 = jnp.zeros((FF,), jnp.float32)
        W2 = _lin(ks[7], FF, (FF, D))
        b2 = jnp.zeros((D,), jnp.float32)
        g1 = jnp.ones((D,), jnp.float32)
        beta1 = jnp.zeros((D,), jnp.float32)
        g2 = jnp.ones((D,), jnp.float32)
        beta2 = jnp.zeros((D,), jnp.float32)
        return dict(src=src, adj_matrix=adj_matrix, Wq=Wq, bq=bq, Wk=Wk, bk=bk, Wv=Wv, bv=bv, Wo=Wo, bo=bo, W1=W1, b1=b1, W2=W2, b2=b2, g1=g1, beta1=beta1, g2=g2, beta2=beta2)
    _L1_gnn_all = _L1_gnn_setup()
    _L1_gnn_in = {k: v for k, v in _L1_gnn_all.items() if k in ('Wq', 'bq', 'Wk', 'bk', 'Wv', 'bv', 'Wo', 'bo', 'W1', 'b1', 'W2', 'b2', 'g1', 'beta1', 'g2', 'beta2', )}
    del _L1_gnn_all

    return {
        "x": x,
        "adj": adj,
        "L0_gnn_W1": _L0_gnn_in["W1"],
        "L0_gnn_a1": _L0_gnn_in["a1"],
        "L0_gnn_W2": _L0_gnn_in["W2"],
        "L0_gnn_a2": _L0_gnn_in["a2"],
        "L0_gnn_w_ff1": _L0_gnn_in["w_ff1"],
        "L0_gnn_b_ff1": _L0_gnn_in["b_ff1"],
        "L0_gnn_w_ff2": _L0_gnn_in["w_ff2"],
        "L0_gnn_b_ff2": _L0_gnn_in["b_ff2"],
        "L0_gnn_g_ln1": _L0_gnn_in["g_ln1"],
        "L0_gnn_b_ln1": _L0_gnn_in["b_ln1"],
        "L0_gnn_g_ln2": _L0_gnn_in["g_ln2"],
        "L0_gnn_b_ln2": _L0_gnn_in["b_ln2"],
        "L1_gnn_Wq": _L1_gnn_in["Wq"],
        "L1_gnn_bq": _L1_gnn_in["bq"],
        "L1_gnn_Wk": _L1_gnn_in["Wk"],
        "L1_gnn_bk": _L1_gnn_in["bk"],
        "L1_gnn_Wv": _L1_gnn_in["Wv"],
        "L1_gnn_bv": _L1_gnn_in["bv"],
        "L1_gnn_Wo": _L1_gnn_in["Wo"],
        "L1_gnn_bo": _L1_gnn_in["bo"],
        "L1_gnn_W1": _L1_gnn_in["W1"],
        "L1_gnn_b1": _L1_gnn_in["b1"],
        "L1_gnn_W2": _L1_gnn_in["W2"],
        "L1_gnn_b2": _L1_gnn_in["b2"],
        "L1_gnn_g1": _L1_gnn_in["g1"],
        "L1_gnn_beta1": _L1_gnn_in["beta1"],
        "L1_gnn_g2": _L1_gnn_in["g2"],
        "L1_gnn_beta2": _L1_gnn_in["beta2"],
    }

def reference(x, adj, L0_gnn_W1, L0_gnn_a1, L0_gnn_W2, L0_gnn_a2, L0_gnn_w_ff1, L0_gnn_b_ff1, L0_gnn_w_ff2, L0_gnn_b_ff2, L0_gnn_g_ln1, L0_gnn_b_ln1, L0_gnn_g_ln2, L0_gnn_b_ln2, L1_gnn_Wq, L1_gnn_bq, L1_gnn_Wk, L1_gnn_bk, L1_gnn_Wv, L1_gnn_bv, L1_gnn_Wo, L1_gnn_bo, L1_gnn_W1, L1_gnn_b1, L1_gnn_W2, L1_gnn_b2, L1_gnn_g1, L1_gnn_beta1, L1_gnn_g2, L1_gnn_beta2):
    import jax
    import jax.numpy as jnp
    def _L0_gnn_ref(x, adj, W1, a1, W2, a2, w_ff1, b_ff1, w_ff2, b_ff2, g_ln1, b_ln1, g_ln2, b_ln2):
        import jax, jax.numpy as jnp
        import numpy as np
        ALPHA = 0.2
        NEG = -9000000000000000.0
        EPS = 1e-05

        def _gat(h, adj, W, a, out_features):
            Wh = jnp.matmul(h, W)
            Wh1 = jnp.matmul(Wh, a[:out_features])
            Wh2 = jnp.matmul(Wh, a[out_features:])
            e = Wh1 + jnp.swapaxes(Wh2, 1, 2)
            e = jax.nn.leaky_relu(e, negative_slope=ALPHA)
            scores = jnp.where(adj > 0, e, NEG)
            att = jax.nn.softmax(scores, axis=1)
            return jnp.matmul(att, Wh)

        def _layernorm(x, g, b):
            mu = jnp.mean(x, axis=-1, keepdims=True)
            var = jnp.var(x, axis=-1, keepdims=True)
            return (x - mu) * jax.lax.rsqrt(var + EPS) * g + b
        Fout = W1.shape[1]
        residual = x
        h = _gat(x, adj, W1, a1, Fout)
        h = _gat(h, adj, W2, a2, W2.shape[1])
        h = _layernorm(residual + h, g_ln1, b_ln1)
        residual2 = h
        ff = jnp.matmul(jax.nn.relu(jnp.matmul(h, w_ff1) + b_ff1), w_ff2) + b_ff2
        return _layernorm(residual2 + ff, g_ln2, b_ln2)

    def _L1_gnn_ref(src, adj_matrix, Wq, bq, Wk, bk, Wv, bv, Wo, bo, W1, b1, W2, b2, g1, beta1, g2, beta2):
        import jax, jax.numpy as jnp
        import numpy as np
        B, N, D = (8, 1024, 256)
        H = 8
        DH = D // H
        R = 4
        FF = 1024
        EPS = 1e-05

        def _lin(k, fan_in, shape):
            return jax.random.normal(k, shape, jnp.float32) * (1.0 / np.sqrt(fan_in))

        def _ln(x, g, b):
            m = x.mean(-1, keepdims=True)
            v = ((x - m) ** 2).mean(-1, keepdims=True)
            return (x - m) * jax.lax.rsqrt(v + EPS) * g + b
        Bb, Nn, Dm = src.shape
        h, dh = (H, Dm // H)
        q = (src @ Wq + bq).reshape(Bb, Nn, h, dh).transpose(0, 2, 1, 3)
        k = (src @ Wk + bk).reshape(Bb, Nn, h, dh).transpose(0, 2, 1, 3)
        scores = jnp.einsum('bhid,bhjd->bhij', q, k) / np.sqrt(dh)
        attn = jax.nn.softmax(scores, axis=-1)
        out = jnp.zeros_like(q)
        for r in range(Wv.shape[0]):
            v_r = (src @ Wv[r] + bv[r]).reshape(Bb, Nn, h, dh).transpose(0, 2, 1, 3)
            mask = (adj_matrix == r)[:, None]
            out = out + jnp.einsum('bhij,bhjd->bhid', attn * mask, v_r)
        attn_out = out.transpose(0, 2, 1, 3).reshape(Bb, Nn, Dm) @ Wo + bo
        x = _ln(src + attn_out, g1, beta1)
        ff = jax.nn.gelu(x @ W1 + b1, approximate=False) @ W2 + b2
        return _ln(x + ff, g2, beta2)

    x = _L0_gnn_ref(x, adj, L0_gnn_W1, L0_gnn_a1, L0_gnn_W2, L0_gnn_a2, L0_gnn_w_ff1, L0_gnn_b_ff1, L0_gnn_w_ff2, L0_gnn_b_ff2, L0_gnn_g_ln1, L0_gnn_b_ln1, L0_gnn_g_ln2, L0_gnn_b_ln2)
    x = _L1_gnn_ref(x, adj, L1_gnn_Wq, L1_gnn_bq, L1_gnn_Wk, L1_gnn_bk, L1_gnn_Wv, L1_gnn_bv, L1_gnn_Wo, L1_gnn_bo, L1_gnn_W1, L1_gnn_b1, L1_gnn_W2, L1_gnn_b2, L1_gnn_g1, L1_gnn_beta1, L1_gnn_g2, L1_gnn_beta2)
    return x


_drawn_inputs = setup_inputs


def setup_inputs(seed=0):
    import zlib

    import numpy as np

    out = dict(_drawn_inputs(seed))
    spreads = {'L0_gnn_b_ff1': (0.0, 0.1),
     'L0_gnn_b_ff2': (0.0, 0.1),
     'L0_gnn_g_ln1': (1.0, 0.2),
     'L0_gnn_b_ln1': (0.0, 0.1),
     'L0_gnn_g_ln2': (1.0, 0.2),
     'L0_gnn_b_ln2': (0.0, 0.1),
     'L1_gnn_bq': (0.0, 0.8),
     'L1_gnn_bk': (0.0, 0.8),
     'L1_gnn_bv': (0.0, 0.1),
     'L1_gnn_bo': (0.0, 0.1),
     'L1_gnn_b1': (0.0, 0.1),
     'L1_gnn_b2': (0.0, 0.1),
     'L1_gnn_g1': (1.0, 0.2),
     'L1_gnn_beta1': (0.0, 0.1),
     'L1_gnn_g2': (1.0, 0.2),
     'L1_gnn_beta2': (0.0, 0.1)}
    factors = {}
    for name, (base, spread) in spreads.items():
        noise = np.random.default_rng([zlib.crc32(name.encode()), seed]).standard_normal(out[name].shape)
        drawn = base * np.exp(spread * noise) if base else spread * noise
        out[name] = jnp.asarray(drawn.astype(out[name].dtype))
    for name, factor in factors.items():
        out[name] = (out[name] * factor).astype(out[name].dtype)
    return out
```

```python
import concourse.bass as bass
from concourse import mybir
from contextlib import ExitStack


class Event:

    def __init__(self, sem, per_graph):
        self.sem, self.per_graph = sem, per_graph

    def __call__(self, g, n):
        return self.sem, g * self.per_graph + n


def adj_seq_kernel(nc: bass.Bass, x, xT, adjT, p0, p1, out):
    f32, f32r, bf16, i32 = mybir.dt.float32, mybir.dt.float32r, mybir.dt.bfloat16, mybir.dt.int32
    ALU, ACT, AX = mybir.AluOpType, mybir.ActivationFunctionType, mybir.AxisListType

    B, N, D = x.shape
    P = 128
    C = D // P
    assert N == D == C * P
    U = p0["w_ff1"].shape[1]
    UC = U // P
    R = p1["Wv"].shape[0]
    H = 8
    DH = D // H
    HG = P // DH
    SCALE = 1.0 / float(DH) ** 0.5
    ALPHA, NEG, EPS = 0.2, -9000000000000000.0, 1e-5
    WE = D + 2

    ctx = ExitStack()
    with ctx:
        def sb(name, shape, dt=f32, c=ctx):
            return c.enter_context(nc.sbuf_tensor(name, shape, dt))

        def pair(name, shape, c=ctx):
            return sb(name + "_hi", shape, f32r, c), sb(name + "_lo", shape, f32r, c)

        def ps(name, shape):
            return ctx.enter_context(nc.psum_tensor(name, shape, f32))

        def event(name, per_graph):
            return Event(ctx.enter_context(nc.semaphore(name)), per_graph)

        def value(t):
            return t.bitcast(f32)

        gat_w = [pair(f"gat_w{l}", [P, C, WE]) for l in range(2)]
        gat_a = [pair(f"gat_a{l}", [P, C, P]) for l in range(2)]
        up_w = [pair(f"up_w{l}", [P, C, U]) for l in range(2)]
        down_w = [pair(f"down_w{l}", [P, UC, D]) for l in range(2)]
        q_w, k_w, o_w = pair("q_w", [P, C, D]), pair("k_w", [P, C, D]), pair("o_w", [P, C, D])
        v_w = pair("v_w", [P, C, R * D])
        v_bias = sb("v_bias", [P, R * D])
        gain_row = [sb(f"gain_row{n}", [P, D]) for n in range(4)]
        shift_row = [sb(f"shift_row{n}", [P, D]) for n in range(4)]
        gain_col = [sb(f"gain_col{n}", [P, C]) for n in range(3)]
        shift_col = [sb(f"shift_col{n}", [P, C]) for n in range(3)]
        up_bias = [sb(f"up_bias{l}", [P, UC]) for l in range(2)]
        qk_bias = sb("qk_bias", [P, 2, C])
        ident = sb("ident", [P, P])
        neg_half = sb("neg_half", [P, C])

        raw_ctx = ExitStack()
        raw_gat = [sb(f"raw_gat{l}", [P, C, WE], c=raw_ctx) for l in range(2)]
        raw_a = [sb(f"raw_a{l}", [P, 2 * D], c=raw_ctx) for l in range(2)]
        raw_arep = [sb(f"raw_arep{l}", [P, C, P], c=raw_ctx) for l in range(2)]
        raw_prod = sb("raw_prod", [P, 2, 2, C, D], c=raw_ctx)
        raw_wa = sb("raw_wa", [P, 2, C], c=raw_ctx)
        raw_up = [sb(f"raw_up{l}", [P, C, U], c=raw_ctx) for l in range(2)]
        raw_down = [sb(f"raw_down{l}", [P, UC, D], c=raw_ctx) for l in range(2)]
        raw_qko = [sb(f"raw_{n}", [P, C, D], c=raw_ctx) for n in "qko"]
        raw_v = sb("raw_v", [P, C, R * D], c=raw_ctx)
        raw_next = [sb(f"raw_next{n}", [P, D], c=raw_ctx) for n in range(3)]
        raw_ctx.close()

        xT_in = sb("xT_in", [P, C, N])
        x_in = sb("x_in", [P, C, D])
        adj0_in = sb("adj0_in", [P, C, N], i32)
        fence = sb("fence", [P, C, N])
        gT = pair("gT", [P, C, N])
        gat_ctx = ExitStack()
        pre = sb("pre", [P, C, N], c=gat_ctx)
        score = sb("score", [P, C, N], c=gat_ctx)
        att = sb("att", [P, C, N], c=gat_ctx)
        att_s = pair("att_s", [P, C, N], gat_ctx)
        wh_s = pair("wh_s", [P, C, D], gat_ctx)
        gat_ctx.close()
        masked = sb("masked", [P, 2, HG, C * N])
        wh2 = sb("wh2", [P, C])
        g_max, g_nmax = sb("g_max", [P, C]), sb("g_nmax", [P, C])
        g_sum, g_rec = sb("g_sum", [P, C]), sb("g_rec", [P, C])
        norm = [sb(f"norm{n}", [P, C, D]) for n in range(4)]
        res = [sb(f"res{n}", [P, C, D]) for n in range(4)]
        stats = [sb(f"stats{n}", [P, C, 6]) for n in range(4)]
        meanvar = [sb(f"meanvar{n}", [P, C, 2]) for n in range(4)]
        vareps = [sb(f"vareps{n}", [P, C]) for n in range(4)]
        rstd = [sb(f"rstd{n}", [P, C]) for n in range(4)]
        hT_full = sb("hT_full", [P, C, N])
        ao_ctx = ExitStack()
        ao = pair("ao", [P, C, N], ao_ctx)
        ao_ctx.close()
        hT = [pair(f"hT{n}", [P, C, N]) for n in (2, 0, 1)]
        hT = [hT[1], hT[2], hT[0]]
        hid_full = sb("hid_full", [P, 2, 2, N])
        hid = pair("hid", [P, UC, N])
        adj1_in = sb("adj1_in", [P, C, N], i32)
        is_rel = sb("is_rel", [P, R, C * N], bf16)
        qk = sb("qk", [P, 2, C, N])
        v_sb = sb("v_sb", [P, C, R * D])
        prob = sb("prob", [P, HG, C, N])
        s_max, s_nmax = sb("s_max", [P, 2 * HG * C]), sb("s_nmax", [P, 2 * HG * C])
        s_sum, s_rec = sb("s_sum", [P, 2 * HG * C]), sb("s_rec", [P, 2 * HG * C])

        ps0 = ps("ps0", [P, 3, 512])
        ps_ao = ps("ps_ao", [P, 1, 512])
        ps1 = ps("ps1", [P, 4, 512])

        params_in = event("params_in", 0)
        prep_v = event("prep_v", 0)
        prep_p = event("prep_p", 0)
        gate_v = event("gate_v", 0)
        xT_loaded, x_loaded = event("xT_loaded", 16), event("x_loaded", 16)
        adj0_loaded, adj1_loaded = event("adj0_loaded", 16), event("adj1_loaded", 16)
        x_hi, x_lo = event("x_hi", 1), event("x_lo", 1)
        fence_set = event("fence_set", 1)
        wh_done = event("wh_done", 6)
        wh2_set = event("wh2_set", 2)
        pre_set = event("pre_set", 4)
        score_set = event("score_set", 2)
        g_max_set = event("g_max_set", 4)
        g_nmax_set = event("g_nmax_set", 2)
        att_set = event("att_set", 4)
        g_rec_set = event("g_rec_set", 2)
        whs_hi, whs_lo = event("whs_hi", 4), event("whs_lo", 4)
        att_hi, att_lo = event("att_hi", 2), event("att_lo", 2)
        mix_done = event("mix_done", 2)
        h1_hi, h1_lo = event("h1_hi", 1), event("h1_lo", 1)
        ysum = [event(f"ysum{n}", 1) for n in range(4)]
        stat_set = [event(f"stat_set{n}", 2) for n in range(4)]
        mv_set = [event(f"mv_set{n}", 2) for n in range(4)]
        ve_set = [event(f"ve_set{n}", 1) for n in range(4)]
        rstd_set = [event(f"rstd_set{n}", 1) for n in range(4)]
        norm_set = [event(f"norm_set{n}", 2) for n in range(4)]
        res_set = [event(f"res_set{n}", 2) for n in range(4)]
        turned = [event(f"turned{n}", 1) for n in range(3)]
        hT_set = [event(f"hT_set{n}", 2) for n in range(3)]
        hT_hi = [event(f"hT_hi{n}", 1) for n in range(3)]
        hT_lo = [event(f"hT_lo{n}", 1) for n in range(3)]
        up_done = [event(f"up_done{l}", UC // 2) for l in range(2)]
        hid_set = [event(f"hid_set{l}", UC) for l in range(2)]
        hid_hi = [event(f"hid_hi{l}", UC // 2) for l in range(2)]
        hid_lo = [event(f"hid_lo{l}", UC // 2) for l in range(2)]
        down_done = [event(f"down_done{l}", 1) for l in range(2)]
        rel_set = event("rel_set", R)
        qk_done, qk_set = event("qk_done", 2), event("qk_set", 4)
        v_done, v_set = event("v_done", 4), event("v_set", 4)
        s_done = event("s_done", 2 * HG)
        s_max_set, s_nmax_set = event("s_max_set", 4), event("s_nmax_set", 4)
        prob_set = event("prob_set", 4 * HG)
        s_rec_set = event("s_rec_set", 4)
        prob_scaled = event("prob_scaled", 4)
        prob_turned = event("prob_turned", 2 * HG)
        masked_set = event("masked_set", 4 * R)
        av_done = event("av_done", 2 * R)
        ao_hi, ao_lo = event("ao_hi", 2), event("ao_lo", 2)
        wo_done = event("wo_done", 1)
        stored = event("stored", 16)

        def chunk(t, c):
            return t[:, c, :]

        def sp_body(sp, t, gat, att1):
            if gat:
                c = t + 2
                if not isinstance(t, int) or c > 0:
                    sp.wait_ge(*x_lo(c - 1, 1))
                sp.dma_start(xT_in[:], xT[c].rearrange("(k p) n -> p k n", p=P)).then_inc(xT_loaded.sem, 16)
                if not isinstance(t, int) or c > 0:
                    sp.wait_ge(*fence_set(c - 1, 1))
                sp.dma_start(adj0_in[:], adjT[c].rearrange("(k p) n -> p k n", p=P)).then_inc(adj0_loaded.sem, 16)
                if not isinstance(t, int) or c > 0:
                    sp.wait_ge(*ysum[0](c - 1, 1))
                sp.dma_start(x_in[:], x[c].rearrange("(k p) n -> p k n", p=P)).then_inc(x_loaded.sem, 16)
            if not isinstance(t, int) or -1 <= t < B - 1:
                if not isinstance(t, int) or t >= 0:
                    sp.wait_ge(*rel_set(t, R))
                sp.dma_start(adj1_in[:], adjT[t + 1].rearrange("(k p) n -> p k n", p=P)).then_inc(adj1_loaded.sem, 16)
            if att1:
                sp.wait_ge(*res_set[3](t, 2))
                sp.dma_start(out[t].rearrange("(k p) n -> p k n", p=P), res[3][:]).then_inc(stored.sem, 16)

        def product(ps_out, left, right, first, last):
            nc.tensor.matmul(ps_out, left[0], right[0], start=first, stop=False)
            nc.tensor.matmul(ps_out, left[0], right[1], start=False, stop=False)
            return nc.tensor.matmul(ps_out, left[1], right[0], start=False, stop=last)

        def cut(halves, *index):
            return tuple(h[(slice(None), *index)] for h in halves)

        def nodes(c):
            return slice(c * P, (c + 1) * P)

        def pe_gat_project(pe, g, l):
            if l == 0:
                pe.wait_ge(*x_hi(g, 1))
                pe.wait_ge(*x_lo(g, 1))
                if not isinstance(g, int) or g > 0:
                    if not isinstance(g, int) or g > 1:
                        pe.wait_ge(*hT_set[1](g - 2, 2))
            else:
                pe.wait_ge(*h1_hi(g, 1))
                pe.wait_ge(*h1_lo(g, 1))
            for i in range(C):
                for k in range(C):
                    last = product(ps0[:, i, 0:WE], cut(gT, k, nodes(i)), cut(gat_w[l], k), k == 0, k == C - 1)
                last.then_inc(wh_done.sem, 1)
            for k in range(C):
                last = product(ps0[:, 2, 0:N], cut(gat_a[l], k), cut(gT, k), k == 0, k == C - 1)
            last.then_inc(wh_done.sem, 1)

        def pe_gat_mix(pe, g, l):
            pe.wait_ge(*whs_lo(g, 2 * l + 2))
            pe.wait_ge(*att_lo(g, l + 1))
            left, right = (wh_s, att_s) if l == 0 else (att_s, wh_s)
            for i in range(C):
                for k in range(C):
                    last = product(ps0[:, 2, i * 256:(i + 1) * 256], cut(left, k, nodes(i)), cut(right, k),
                                   k == 0, k == C - 1)
            last.then_inc(mix_done.sem, 1)

        def pe_turn(pe, g, n, bank):
            pe.wait_ge(*norm_set[n](g, 2))
            for i in range(C):
                for f in range(C):
                    last = nc.tensor.transpose(bank[:, f * N + i * P:f * N + (i + 1) * P],
                                               norm[n][:, i, nodes(f)], ident[:])
            last.then_inc(turned[n].sem, 1)

        ff_in = [0, 2]
        ff_bank = [[ps0[:, m, :] for m in (0, 1, 2, 0)], [ps1[:, m, :] for m in (1, 2, 3, 0)]]
        ff_out = [ps0[:, 1, :], ps_ao[:, 0, :]]

        def pe_up(pe, g, l, pairs):
            for m in pairs:
                if m == 0:
                    pe.wait_ge(*hT_hi[ff_in[l]](g, 1))
                    pe.wait_ge(*hT_lo[ff_in[l]](g, 1))
                if m == 3 and l == 0:
                    pe.wait_ge(*hid_set[l](g, 2))
                for u in range(2):
                    for k in range(C):
                        last = product(ff_bank[l][m][:, u * N:(u + 1) * N], cut(up_w[l], k, nodes(2 * m + u)),
                                       cut(hT[ff_in[l]], k), k == 0, k == C - 1)
                last.then_inc(up_done[l].sem, 1)

        def pe_down(pe, g, l, i):
            if i == 0 and l == 0:
                pe.wait_ge(*hid_set[0](g, 4))
            for k in range(UC):
                if i == 0 and k % 2 == 0:
                    pe.wait_ge(*hid_lo[l](g, k // 2 + 1))
                last = product(ff_out[l][:, i * D:(i + 1) * D], cut(hid, k, nodes(i)), cut(down_w[l], k),
                               k == 0, k == UC - 1)
            if i == C - 1:
                last.then_inc(down_done[l].sem, 1)

        def pe_qk(pe, g):
            pe.wait_ge(*hT_hi[1](g, 1))
            pe.wait_ge(*hT_lo[1](g, 1))
            for b, w in enumerate((q_w, k_w)):
                for c in range(C):
                    for k in range(C):
                        last = product(ps1[:, b, c * N:(c + 1) * N], cut(w, k, nodes(c)), cut(hT[1], k),
                                       k == 0, k == C - 1)
                last.then_inc(qk_done.sem, 1)

        V_PARTS = [(0, 0, 2), (0, 1, 3), (1, 0, 0), (1, 1, 1)]

        def pe_v(pe, g):
            for j, rr, b in V_PARTS:
                if b < 2:
                    pe.wait_ge(*qk_set(g, 2 * b + 2))
                for k in range(C):
                    last = product(ps1[:, b, :], cut(hT[1], k, nodes(j)), cut(v_w, k, slice(rr * 512, rr * 512 + 512)),
                                   k == 0, k == C - 1)
                last.then_inc(v_done.sem, 1)

        def pe_scores(pe, g, hg):
            if hg == 0:
                pe.wait_ge(*v_set(g, 4))
            else:
                pe.wait_ge(*masked_set(g, 2 * R))
            for h in range(HG):
                rows = slice(h * DH, (h + 1) * DH)
                for i in range(C):
                    last = nc.tensor.matmul(ps1[:, h, i * N:(i + 1) * N], qk[rows, 0, hg, nodes(i)],
                                            qk[rows, 1, hg, :], start=True, stop=True)
                last.then_inc(s_done.sem, 1)

        def pe_prob_turn(pe, g, hg):
            for h in range(HG):
                if h % 2 == 0:
                    pe.wait_ge(*prob_scaled(g, 2 * hg + h // 2 + 1))
                for i in range(C):
                    for j in range(C):
                        last = nc.tensor.transpose(ps1[:, h, j * N + i * P:j * N + (i + 1) * P],
                                                   prob[:, h, i, nodes(j)], ident[:])
                last.then_inc(prob_turned.sem, 1)

        def pe_av(pe, g, hg, r):
            if hg == 1 and r == 0:
                pe.wait_ge(*ao_lo(g, 1))
            pe.wait_ge(*masked_set(g, 2 * (hg * R + r) + 2))
            for j in range(C):
                for h in range(HG):
                    col = r * D + hg * P + h * DH
                    last = nc.tensor.matmul(ps_ao[h * DH:(h + 1) * DH, 0, hg * N:(hg + 1) * N],
                                            v_sb[:, j, col:col + DH],
                                            masked[:, r % 2, h, j * N:(j + 1) * N],
                                            start=(r == 0 and j == 0), stop=(r == R - 1 and j == C - 1))
            last.then_inc(av_done.sem, 1)

        def pe_wo(pe, g):
            pe.wait_ge(*ao_lo(g, 2))
            for i in range(C):
                for k in range(C):
                    last = product(ps1[:, 0, i * D:(i + 1) * D], cut(ao, k, nodes(i)), cut(o_w, k), k == 0, k == C - 1)
            last.then_inc(wo_done.sem, 1)

        def pe_body(pe, t, gat, ff0, att1):
            a, b, c = t + 1, t, t + 2
            if att1:
                pe_qk(pe, b)
            if ff0:
                pe_up(pe, a, 0, (0, 1))
            if att1:
                pe_v(pe, b)
                pe_scores(pe, b, 0)
            if ff0:
                pe_up(pe, a, 0, (2, 3))
            if att1:
                pe_prob_turn(pe, b, 0)
                for r in range(R):
                    pe_av(pe, b, 0, r)
                pe_scores(pe, b, 1)
            if ff0:
                for i in range(C):
                    pe_down(pe, a, 0, i)
            if att1:
                pe_prob_turn(pe, b, 1)
                for r in range(R):
                    pe_av(pe, b, 1, r)
            if ff0:
                pe_turn(pe, a, 1, ps0[:, 2, :])
            if att1:
                pe_wo(pe, b)
            if gat:
                pe_gat_project(pe, c, 0)
            if att1:
                pe_turn(pe, b, 2, ps1[:, 1, :])
                pe_up(pe, b, 1, (0, 1))
            if gat:
                pe_gat_mix(pe, c, 0)
            if att1:
                pe_up(pe, b, 1, (2, 3))
            if gat:
                pe_gat_project(pe, c, 1)
            if att1:
                pe_down(pe, b, 1, 0)
            if gat:
                pe_gat_mix(pe, c, 1)
            if att1:
                pe_down(pe, b, 1, 1)
            if gat:
                pe_turn(pe, c, 0, ps0[:, 0, :])

        def act_gat_pre(act, g, l):
            act.wait_ge(*wh_done(g, 3 * l + 3))
            act.wait_ge(*wh2_set(g, l + 1))
            for j in range(C):
                act.activation(pre[:, j, :], ps0[:, 2, 0:N], ACT.Identity, bias=wh2[:, j:j + 1]).then_inc(pre_set.sem, 1)

        def act_gat_exp(act, g, l):
            act.wait_ge(*g_nmax_set(g, l + 1))
            for j in range(C):
                act.activation(att[:, j, :], score[:, j, :], ACT.Exp, bias=g_nmax[:, j:j + 1],
                               accum_out=g_sum[:, j:j + 1]).then_inc(att_set.sem, 1)

        def act_h1(act, g):
            act.wait_ge(*mix_done(g, 1))
            act.activation(gT[0][:].rearrange("p c n -> p (c n)"), ps0[:, 2, :], ACT.Copy).then_inc(h1_hi.sem, 1)

        def act_turned(act, g, n, bank):
            act.wait_ge(*turned[n](g, 1))
            for f in range(C):
                act.activation(hT_full[:, f, :], bank[:, f * N:(f + 1) * N], ACT.Identity,
                               bias=shift_col[n][:, f:f + 1], scale=gain_col[n][:, f:f + 1]).then_inc(hT_set[n].sem, 1)
            act.wait_ge(*hT_set[n](g, 2))
            act.activation(hT[n][0][:], hT_full[:], ACT.Copy).then_inc(hT_hi[n].sem, 1)

        def act_hidden(act, g, l, pairs):
            for m in pairs:
                act.wait_ge(*up_done[l](g, m + 1))
                if m >= 2:
                    act.wait_ge(*hid_lo[l](g, m - 1))
                for u in range(2):
                    act.activation(hid_full[:, m % 2, u, :], ff_bank[l][m][:, u * N:(u + 1) * N],
                                   ACT.Relu if l == 0 else ACT.Gelu,
                                   bias=up_bias[l][:, 2 * m + u:2 * m + u + 1]).then_inc(hid_set[l].sem, 1)
                act.wait_ge(*hid_set[l](g, 2 * m + 2))
                act.activation(hid[0][:, 2 * m:2 * m + 2, :], hid_full[:, m % 2, :, :], ACT.Copy).then_inc(hid_hi[l].sem, 1)

        def act_qk(act, g):
            for b in range(2):
                act.wait_ge(*qk_done(g, b + 1))
                for c in range(C):
                    act.activation(qk[:, b, c, :], ps1[:, b, c * N:(c + 1) * N], ACT.Identity,
                                   bias=qk_bias[:, b, c:c + 1]).then_inc(qk_set.sem, 1)

        def act_prob(act, g, hg):
            for h in range(HG):
                if h % 2 == 0:
                    act.wait_ge(*s_nmax_set(g, 2 * hg + h // 2 + 1))
                for i in range(C):
                    col = (hg * HG + h) * C + i
                    act.activation(prob[:, h, i, :], ps1[:, h, i * N:(i + 1) * N], ACT.Exp,
                                   bias=s_nmax[:, col:col + 1], scale=SCALE,
                                   accum_out=s_sum[:, col:col + 1]).then_inc(prob_set.sem, 1)

        def act_ao(act, g, hg):
            act.wait_ge(*av_done(g, (hg + 1) * R))
            act.activation(ao[0][:, hg, :], ps_ao[:, 0, hg * N:(hg + 1) * N], ACT.Copy).then_inc(ao_hi.sem, 1)

        def act_body(act, t, gat, ff0, att1):
            a, b, c = t + 1, t, t + 2
            if att1:
                act_qk(act, b)
            if ff0:
                act_hidden(act, a, 0, (0, 1))
            if att1:
                act_prob(act, b, 0)
            if ff0:
                act_hidden(act, a, 0, (2, 3))
            if att1:
                act_ao(act, b, 0)
                act_prob(act, b, 1)
            if ff0:
                act_turned(act, a, 1, ps0[:, 2, :])
            if att1:
                act_ao(act, b, 1)
            if gat:
                act_gat_pre(act, c, 0)
                act_gat_exp(act, c, 0)
            if att1:
                act_turned(act, b, 2, ps1[:, 1, :])
            if gat:
                act_h1(act, c)
                act_gat_pre(act, c, 1)
                act_gat_exp(act, c, 1)
            if att1:
                act_hidden(act, b, 1, (0, 1, 2, 3))
            if gat:
                act_turned(act, c, 0, ps0[:, 0, :])

        def dve_gat_in(dve, g):
            dve.wait_ge(*xT_loaded(g, 16))
            dve.tensor_copy(gT[0][:], xT_in[:]).then_inc(x_hi.sem, 1)
            dve.wait_ge(*adj0_loaded(g, 16))
            dve.tensor_scalar(fence[:], adj0_in[:], 0.0, NEG, ALU.is_le, ALU.mult).then_inc(fence_set.sem, 1)

        def dve_gat_score(dve, g, l):
            dve.wait_ge(*wh_done(g, 3 * l + 2))
            dve.tensor_copy(wh2[:].unsqueeze(2), ps0[:, 0:C, D:D + 1]).then_inc(wh2_set.sem, 1)
            dve.wait_ge(*pre_set(g, 2 * l + 2))
            dve.scalar_tensor_tensor(out=score[:], in0=pre[:], scalar=ALPHA, in1=pre[:],
                                     op0=ALU.mult, op1=ALU.max).then_inc(score_set.sem, 1)
            dve.wait_ge(*score_set(g, l + 1))
            if l == 0:
                dve.wait_ge(*fence_set(g, 1))
            dve.sem_inc(gate_v.sem, 1)
            for j in range(C):
                dve.tensor_tensor_reduce(out=score[:, j, :], in0=score[:, j, :], in1=fence[:, j, :], scale=1.0,
                                         scalar=-3.0e38, op0=ALU.add, op1=ALU.max,
                                         accum_out=g_max[:, j:j + 1]).then_inc(g_max_set.sem, 1)
            dve.wait_ge(*g_max_set(g, 2 * l + 2))
            dve.tensor_scalar(g_nmax[:], g_max[:], -1.0, None, ALU.mult).then_inc(g_nmax_set.sem, 1)

        def dve_gat_split(dve, g, l):
            dve.wait_ge(*att_set(g, 2 * l + 2))
            dve.reciprocal(g_rec[:], g_sum[:]).then_inc(g_rec_set.sem, 1)
            dve.tensor_copy(att_s[0][:], att[:]).then_inc(att_hi.sem, 1)
            dve.wait_ge(*g_rec_set(g, l + 1))
            for j in range(C):
                dve.tensor_scalar(wh_s[0][:, j, :], ps0[:, j, 0:D], g_rec[:, j:j + 1], None,
                                  ALU.mult).then_inc(whs_hi.sem, 1)
            dve.wait_ge(*att_hi(g, l + 1))
            dve.tensor_tensor(att_s[1][:], att[:], value(att_s[0][:]), ALU.subtract).then_inc(att_lo.sem, 1)
            dve.wait_ge(*whs_hi(g, 2 * l + 2))
            for j in range(C):
                dve.scalar_tensor_tensor(out=wh_s[1][:, j, :], in0=ps0[:, j, 0:D], scalar=g_rec[:, j:j + 1],
                                         in1=value(wh_s[0][:, j, :]), op0=ALU.mult,
                                         op1=ALU.subtract).then_inc(whs_lo.sem, 1)

        def dve_h1(dve, g):
            dve.wait_ge(*h1_hi(g, 1))
            dve.tensor_tensor(gT[1][:].rearrange("p c n -> p (c n)"), ps0[:, 2, :],
                              value(gT[0][:]).rearrange("p c n -> p (c n)"), ALU.subtract).then_inc(h1_lo.sem, 1)

        ln_bank = [ps0[:, 2, :], ps0[:, 1, :], ps1[:, 0, :], ps_ao[:, 0, :]]
        ln_done = [lambda g: mix_done(g, 2), lambda g: down_done[0](g, 1), lambda g: wo_done(g, 1),
                   lambda g: down_done[1](g, 1)]

        def dve_norm(dve, g, n):
            dve.wait_ge(*ln_done[n](g))
            dve.wait_ge(*(x_loaded(g, 16) if n == 0 else res_set[n - 1](g, 2)))
            residual = x_in if n == 0 else res[n - 1]
            y = norm[n]
            dve.tensor_tensor(y[:].rearrange("p c n -> p (c n)"), ln_bank[n],
                              residual[:].rearrange("p c n -> p (c n)"), ALU.add).then_inc(ysum[n].sem, 1)
            dve.wait_ge(*ysum[n](g, 1))
            for i in range(C):
                dve.bn_stats(stats[n][:, i, :], y[:, i, :]).then_inc(stat_set[n].sem, 1)
            dve.wait_ge(*stat_set[n](g, 2))
            dve.sem_inc(gate_v.sem, 1)
            for i in range(C):
                dve.bn_aggr(meanvar[n][:, i, :], stats[n][:, i, :]).then_inc(mv_set[n].sem, 1)
            dve.wait_ge(*mv_set[n](g, 2))
            dve.tensor_scalar(vareps[n][:].unsqueeze(2), meanvar[n][:, :, 1:2], EPS, None, ALU.add).then_inc(ve_set[n].sem, 1)

        def dve_norm_end(dve, g, n):
            dve.wait_ge(*rstd_set[n](g, 1))
            for i in range(C):
                dve.tensor_scalar(norm[n][:, i, :], norm[n][:, i, :], meanvar[n][:, i, 0:1], rstd[n][:, i:i + 1],
                                  ALU.subtract, ALU.mult).then_inc(norm_set[n].sem, 1)

        def dve_relations(dve, g):
            dve.wait_ge(*adj1_loaded(g, 16))
            for r in range(R):
                dve.tensor_scalar(is_rel[:, r, :], adj1_in[:].rearrange("p c n -> p (c n)"), float(r), None,
                                  ALU.is_equal).then_inc(rel_set.sem, 1)

        def dve_v(dve, g):
            for n, (j, rr, b) in enumerate(V_PARTS):
                dve.wait_ge(*v_done(g, n + 1))
                dve.tensor_tensor(v_sb[:, j, rr * 512:(rr + 1) * 512], ps1[:, b, :], v_bias[:, rr * 512:(rr + 1) * 512],
                                  ALU.add).then_inc(v_set.sem, 1)

        def dve_max(dve, g, hg):
            for m in range(2):
                cols = slice((hg * HG + 2 * m) * C, (hg * HG + 2 * m + 2) * C)
                k = 2 * hg + m + 1
                dve.wait_ge(*s_done(g, hg * HG + 2 * m + 2))
                dve.tensor_reduce(s_max[:, cols], ps1[:, 2 * m:2 * m + 2, :].rearrange("p b (c n) -> p (b c) n", n=N),
                                  AX.X, ALU.max).then_inc(s_max_set.sem, 1)
                dve.wait_ge(*s_max_set(g, k))
                dve.tensor_scalar(s_nmax[:, cols], s_max[:, cols], -SCALE, None, ALU.mult).then_inc(s_nmax_set.sem, 1)

        def dve_rec(dve, g, hg):
            for m in range(2):
                cols = slice((hg * HG + 2 * m) * C, (hg * HG + 2 * m + 2) * C)
                dve.wait_ge(*prob_set(g, C * (hg * HG + 2 * m + 2)))
                dve.reciprocal(s_rec[:, cols], s_sum[:, cols]).then_inc(s_rec_set.sem, 1)

        def dve_mask(dve, g, hg):
            for r in range(R):
                k = hg * R + r
                if r == 0 and hg == 0:
                    dve.wait_ge(*rel_set(g, R))
                if k >= 2:
                    dve.wait_ge(*av_done(g, k - 1))
                for m in range(2):
                    if r == 0:
                        dve.wait_ge(*prob_turned(g, hg * HG + 2 * m + 2))
                    dve.tensor_tensor(masked[:, r % 2, 2 * m:2 * m + 2, :], ps1[:, 2 * m:2 * m + 2, :],
                                      is_rel[:, r:r + 1, :].broadcast_to([P, 2, C * N]),
                                      ALU.mult).then_inc(masked_set.sem, 1)

        def dve_ao(dve, g, hg):
            dve.wait_ge(*ao_hi(g, hg + 1))
            dve.tensor_tensor(ao[1][:, hg, :], ps_ao[:, 0, hg * N:(hg + 1) * N], value(ao[0][:, hg, :]),
                              ALU.subtract).then_inc(ao_lo.sem, 1)

        def dve_body(dve, t, gat, ff0, att1):
            a, b, c = t + 1, t, t + 2
            if att1:
                dve_relations(dve, b)
                dve_v(dve, b)
                dve_max(dve, b, 0)
                dve_rec(dve, b, 0)
                dve_mask(dve, b, 0)
                dve_ao(dve, b, 0)
                dve_max(dve, b, 1)
                dve_rec(dve, b, 1)
            if ff0:
                dve_norm(dve, a, 1)
                dve_norm_end(dve, a, 1)
            if gat:
                dve_gat_in(dve, c)
            if att1:
                dve_mask(dve, b, 1)
                dve_ao(dve, b, 1)
                dve_norm(dve, b, 2)
            if gat:
                dve_gat_score(dve, c, 0)
            if att1:
                dve_norm_end(dve, b, 2)
            if gat:
                dve_gat_split(dve, c, 0)
                dve_h1(dve, c)
                dve_gat_score(dve, c, 1)
                dve_gat_split(dve, c, 1)
                dve_norm(dve, c, 0)
                dve_norm_end(dve, c, 0)
            if att1:
                dve_norm(dve, b, 3)
                dve_norm_end(dve, b, 3)

        def pool_gat_in(pool, g):
            pool.wait_ge(*x_hi(g, 1))
            pool.tensor_tensor(gT[1][:], xT_in[:], value(gT[0][:]), ALU.subtract).then_inc(x_lo.sem, 1)

        def pool_rstd(pool, g, n):
            pool.wait_ge(*ve_set[n](g, 1))
            pool.tensor_tensor(rstd[n][:], vareps[n][:], neg_half[:], ALU.pow).then_inc(rstd_set[n].sem, 1)

        def pool_affine(pool, g, n):
            pool.wait_ge(*norm_set[n](g, 2))
            if n == 3 and (not isinstance(g, int) or g > 0):
                pool.wait_ge(*stored(g - 1, 16))
            pool.tensor_tensor(res[n][:], norm[n][:], gain_row[n][:].unsqueeze(1).broadcast_to([P, C, D]),
                               ALU.mult).then_inc(res_set[n].sem, 1)
            pool.wait_ge(*res_set[n](g, 1))
            pool.tensor_tensor(res[n][:], res[n][:], shift_row[n][:].unsqueeze(1).broadcast_to([P, C, D]),
                               ALU.add).then_inc(res_set[n].sem, 1)

        def pool_hT(pool, g, n):
            pool.wait_ge(*hT_hi[n](g, 1))
            pool.tensor_tensor(hT[n][1][:], hT_full[:], value(hT[n][0][:]), ALU.subtract).then_inc(hT_lo[n].sem, 1)

        def pool_hidden(pool, g, l, pairs):
            for m in pairs:
                pool.wait_ge(*hid_hi[l](g, m + 1))
                pool.tensor_tensor(hid[1][:, 2 * m:2 * m + 2, :], hid_full[:, m % 2, :, :],
                                   value(hid[0][:, 2 * m:2 * m + 2, :]), ALU.subtract).then_inc(hid_lo[l].sem, 1)

        def pool_prob(pool, g, hg):
            for m in range(2):
                first = (hg * HG + 2 * m) * C
                pool.wait_ge(*s_rec_set(g, 2 * hg + m + 1))
                part = prob[:, 2 * m:2 * m + 2, :, :].rearrange("p h c n -> p (h c) n")
                pool.tensor_tensor(part, part, s_rec[:, first:first + 2 * C].unsqueeze(2).broadcast_to([P, 2 * C, N]),
                                   ALU.mult).then_inc(prob_scaled.sem, 1)

        def pool_body(pool, t, gat, ff0, att1):
            a, b, c = t + 1, t, t + 2
            if ff0:
                pool_hidden(pool, a, 0, (0, 1))
            if att1:
                pool_prob(pool, b, 0)
            if ff0:
                pool_hidden(pool, a, 0, (2, 3))
            if att1:
                pool_prob(pool, b, 1)
            if ff0:
                pool_rstd(pool, a, 1)
                pool_hT(pool, a, 1)
            if gat:
                pool_gat_in(pool, c)
            if att1:
                pool_rstd(pool, b, 2)
            if ff0:
                pool_affine(pool, a, 1)
            if att1:
                pool_hT(pool, b, 2)
                pool_affine(pool, b, 2)
                pool_hidden(pool, b, 1, (0, 1, 2, 3))
            if gat:
                pool_rstd(pool, c, 0)
                pool_hT(pool, c, 0)
            if att1:
                pool_rstd(pool, b, 3)
            if gat:
                pool_affine(pool, c, 0)
            if att1:
                pool_affine(pool, b, 3)

        def rows(w):
            return w.rearrange("(k p) n -> p k n", p=P)

        def across(v):
            return v.unsqueeze(0).broadcast_to([P, v.shape[0]])

        loads = [(raw_gat[l][:, :, 0:D], rows(p0[f"W{l + 1}"])) for l in range(2)]
        loads += [(raw_a[l][:], across(p0[f"a{l + 1}"].rearrange("n o -> (n o)"))) for l in range(2)]
        loads += [(raw_up[0][:], rows(p0["w_ff1"])), (raw_down[0][:], rows(p0["w_ff2"]))]
        loads += [(raw_qko[m][:], rows(p1[w])) for m, w in enumerate(("Wq", "Wk", "Wo"))]
        loads += [(raw_v[:, :, r * D:(r + 1) * D], rows(p1["Wv"][r])) for r in range(R)]
        loads += [(v_bias[:, r * D:(r + 1) * D], across(p1["bv"][r])) for r in range(R)]
        loads += [(raw_up[1][:], rows(p1["W1"])), (raw_down[1][:], rows(p1["W2"]))]
        gains = [p0["g_ln1"], p0["g_ln2"], p1["g1"], p1["g2"]]
        shifts = [p0["b_ln1"], p0["b_ln2"], p1["beta1"], p1["beta2"]]
        loads += [(gain_row[n][:], across(gains[n])) for n in range(4)]
        loads += [(shift_row[n][:], across(shifts[n])) for n in range(4)]
        loads += [(raw_next[n][:], across(v)) for n, v in enumerate((p0["b_ff2"], p1["bo"], p1["b2"]))]
        by_feature = [(gain_col[n][:], gains[n]) for n in range(3)] + [(shift_col[n][:], shifts[n]) for n in range(3)]
        by_feature += [(up_bias[0][:], p0["b_ff1"]), (up_bias[1][:], p1["b1"])]
        by_feature += [(qk_bias[:, 0, :], p1["bq"]), (qk_bias[:, 1, :], p1["bk"])]
        ALL_LOADED = 16 * (len(loads) + len(by_feature))

        splits = [(raw_gat[l], gat_w[l]) for l in range(2)] + [(raw_arep[l], gat_a[l]) for l in range(2)]
        splits += [(raw_up[l], up_w[l]) for l in range(2)] + [(raw_down[l], down_w[l]) for l in range(2)]
        splits += [(raw_qko[0], q_w), (raw_qko[1], k_w), (raw_qko[2], o_w), (raw_v, v_w)]
        WA, PLACED = 8, 8 + 6
        HI = PLACED + len(splits)
        PREP_V = HI + len(splits) + 3
        PREP_P = 4

        def sp_setup(sp):
            for dst, src in loads:
                sp.dma_start(dst, src).then_inc(params_in.sem, 16)
            for dst, src in by_feature:
                sp.dma_start(dst, src.rearrange("(c p) -> p c", p=P), allow_slow_non_contiguous=True)\
                  .then_inc(params_in.sem, 16)
            sp.wait_ge(prep_v.sem, PREP_V)

        def dve_setup(dve):
            dve.wait_ge(params_in.sem, ALL_LOADED)
            for l in range(2):
                for half in range(2):
                    for k in range(C):
                        dst = raw_wa[:, l, k:k + 1] if half == 0 else raw_gat[l][:, k, D:D + 1]
                        dve.tensor_tensor_reduce(out=raw_prod[:, l, half, k, :], in0=raw_gat[l][:, k, 0:D],
                                                 in1=raw_a[l][:, half * D:(half + 1) * D], scale=1.0, scalar=0.0,
                                                 op0=ALU.mult, op1=ALU.add, accum_out=dst).then_inc(prep_v.sem, 1)
            for l in range(2):
                dve.memset(raw_gat[l][:, :, D + 1:WE], 0.0).then_inc(prep_v.sem, 1)
            dve.wait_ge(prep_v.sem, WA)
            for l in range(2):
                for k in range(C):
                    dve.tensor_copy(raw_arep[l][:, k, :], raw_wa[:, l, k:k + 1].broadcast_to([P, P])).then_inc(prep_v.sem, 1)
            dve.wait_ge(prep_v.sem, PLACED)
            for raw, (hi, _) in splits:
                dve.tensor_copy(hi[:], raw[:]).then_inc(prep_v.sem, 1)
            dve.wait_ge(prep_v.sem, HI)
            for raw, (hi, lo) in splits:
                dve.tensor_tensor(lo[:], raw[:], value(hi[:]), ALU.subtract).then_inc(prep_v.sem, 1)
            for n in range(3):
                dve.tensor_tensor(shift_row[n][:], shift_row[n][:], raw_next[n][:], ALU.add).then_inc(prep_v.sem, 1)
            dve.wait_ge(prep_v.sem, PREP_V)

        def pool_setup(pool):
            pool.memset(ident[:], 0.0).then_inc(prep_p.sem, 1)
            pool.memset(neg_half[:], -0.5).then_inc(prep_p.sem, 1)
            pool.wait_ge(prep_p.sem, 2)
            pool.affine_select(out=ident[:], in_=ident[:], compare_op=ALU.not_equal, fill=1.0, base=0,
                               pattern=[[-1, P]], channel_multiplier=1).then_inc(prep_p.sem, 2)
            pool.wait_ge(prep_p.sem, PREP_P)
            pool.wait_ge(prep_v.sem, PREP_V)

        def ready(eng):
            eng.wait_ge(prep_v.sem, PREP_V)
            eng.wait_ge(prep_p.sem, PREP_P)

        def run(eng, body):
            body(eng, -2, True, False, False)
            body(eng, -1, True, True, False)
            body(eng, 0, True, True, True)
            with eng.Fori(1, B - 2) as t:
                body(eng, t, True, True, True)
            body(eng, B - 2, False, True, True)
            body(eng, B - 1, False, False, True)

        block = ctx.enter_context(nc.Block())

        @block.sync
        def _(sp):
            sp_setup(sp)
            run(sp, lambda e, t, gat, ff0, att1: sp_body(e, t, gat, att1))
            sp.wait_ge(*stored(B - 1, 16))

        @block.tensor
        def _(pe):
            ready(pe)
            run(pe, pe_body)

        @block.scalar
        def _(act):
            ready(act)
            run(act, act_body)

        @block.vector
        def _(dve):
            dve_setup(dve)
            run(dve, dve_body)

        @block.gpsimd
        def _(pool):
            pool_setup(pool)
            run(pool, pool_body)


_L0 = ["W1", "a1", "W2", "a2", "w_ff1", "b_ff1", "w_ff2", "b_ff2", "g_ln1", "b_ln1", "g_ln2", "b_ln2"]
_L1 = ["Wq", "bq", "Wk", "bk", "Wv", "bv", "Wo", "bo", "W1", "b1", "W2", "b2", "g1", "beta1", "g2", "beta2"]


def kernel(**inputs):
    import numpy as np
    import concourse.bacc as bacc
    from concourse.bass_utils import run_bass_kernel_spmd

    nc = bacc.Bacc("TRN2", target_bir_lowering=False, num_devices=1, dynamic_dma_scratch_size=1024)
    arrays = {}

    def given(name, a):
        a = np.ascontiguousarray(a)
        arrays[name] = a
        return nc.dram_tensor(name, a.shape, mybir.dt.from_np(a.dtype), kind="ExternalInput").ap()

    xs, adj = np.asarray(inputs["x"]), np.asarray(inputs["adj"])
    x = given("x_nodes", xs)
    xT = given("x_features", xs.transpose(0, 2, 1))
    adjT = given("adj_keys", adj.transpose(0, 2, 1))
    p0 = {n: given(f"L0_{n}", inputs[f"L0_gnn_{n}"]) for n in _L0}
    p1 = {n: given(f"L1_{n}", inputs[f"L1_gnn_{n}"]) for n in _L1}
    out = nc.dram_tensor("out_nodes", xs.shape, mybir.dt.float32, kind="ExternalOutput").ap()
    adj_seq_kernel(nc, x, xT, adjT, p0, p1, out)
    r = run_bass_kernel_spmd(nc, [arrays], core_ids=[0])
    return r.results[0]["out_nodes"]
```

```python
import concourse.bass as bass
from concourse import mybir
from contextlib import ExitStack


class Event:

    def __init__(self, sem, per_graph):
        self.sem, self.per_graph = sem, per_graph

    def __call__(self, g, n):
        return self.sem, g * self.per_graph + n


def adj_seq_kernel(nc: bass.Bass, x, xT, adjT, p0, p1, out):
    f32, f32r, bf16, i32 = mybir.dt.float32, mybir.dt.float32r, mybir.dt.bfloat16, mybir.dt.int32
    ALU, ACT, AX = mybir.AluOpType, mybir.ActivationFunctionType, mybir.AxisListType

    B, N, D = x.shape
    P = 128
    C = D // P
    assert N == D == C * P
    U = p0["w_ff1"].shape[1]
    UC = U // P
    R = p1["Wv"].shape[0]
    RA = 2
    H = 8
    DH = D // H
    HG = P // DH
    SCALE = 1.0 / float(DH) ** 0.5
    ALPHA, NEG, EPS = 0.2, -9000000000000000.0, 1e-5
    WE = D + 2

    ctx = ExitStack()
    with ctx:
        def sb(name, shape, dt=f32, c=ctx):
            return c.enter_context(nc.sbuf_tensor(name, shape, dt))

        def pair(name, shape, c=ctx):
            return sb(name + "_hi", shape, f32r, c), sb(name + "_lo", shape, f32r, c)

        def ps(name, shape):
            return ctx.enter_context(nc.psum_tensor(name, shape, f32))

        def event(name, per_graph):
            return Event(ctx.enter_context(nc.semaphore(name)), per_graph)

        def value(t):
            return (t if isinstance(t, bass.AP) else t[:]).bitcast(f32)

        gat_w = [pair(f"gat_w{l}", [P, C, WE]) for l in range(2)]
        gat_a = [pair(f"gat_a{l}", [P, C, P]) for l in range(2)]
        up_w = [pair(f"up_w{l}", [P, C, U]) for l in range(2)]
        down_w = [pair(f"down_w{l}", [P, UC, D]) for l in range(2)]
        q_w, k_w, o_w = pair("q_w", [P, C, D]), pair("k_w", [P, C, D]), pair("o_w", [P, C, D])
        v_w = pair("v_w", [P, C, R * D])
        v_bias = sb("v_bias", [P, R * D])
        gain_row = [sb(f"gain_row{n}", [P, D]) for n in range(4)]
        shift_row = [sb(f"shift_row{n}", [P, D]) for n in range(4)]
        gain_col = [sb(f"gain_col{n}", [P, C]) for n in range(3)]
        shift_col = [sb(f"shift_col{n}", [P, C]) for n in range(3)]
        up_bias = [sb(f"up_bias{l}", [P, UC]) for l in range(2)]
        qk_bias = sb("qk_bias", [P, 2, C])
        ident = sb("ident", [P, P])
        neg_half = sb("neg_half", [P, C])

        raw_ctx = ExitStack()
        raw_gat = [sb(f"raw_gat{l}", [P, C, WE], c=raw_ctx) for l in range(2)]
        raw_a = [sb(f"raw_a{l}", [P, 2 * D], c=raw_ctx) for l in range(2)]
        raw_arep = [sb(f"raw_arep{l}", [P, C, P], c=raw_ctx) for l in range(2)]
        raw_prod = sb("raw_prod", [P, 2, 2, C, D], c=raw_ctx)
        raw_wa = sb("raw_wa", [P, 2, C], c=raw_ctx)
        raw_up = [sb(f"raw_up{l}", [P, C, U], c=raw_ctx) for l in range(2)]
        raw_down = [sb(f"raw_down{l}", [P, UC, D], c=raw_ctx) for l in range(2)]
        raw_qko = [sb(f"raw_{n}", [P, C, D], c=raw_ctx) for n in "qko"]
        raw_v = sb("raw_v", [P, C, R * D], c=raw_ctx)
        raw_next = [sb(f"raw_next{n}", [P, D], c=raw_ctx) for n in range(3)]
        raw_ctx.close()

        xT_in = sb("xT_in", [P, C, N])
        x_in = sb("x_in", [P, C, D])
        adj0_in = sb("adj0_in", [P, C, N], i32)
        fence = value(adj0_in)
        gT = pair("gT", [P, C, N])
        turns_ctx = ExitStack()
        score = sb("score", [P, C, N], c=turns_ctx)
        wh_s = pair("wh_s", [P, C, D], turns_ctx)
        turns_ctx.close()
        prob = [sb(f"prob{hg}", [P, HG, C, N]) for hg in range(2)]
        att_s = pair("att_s", [P, C, N], turns_ctx)
        turns_ctx.close()
        qk = sb("qk", [P, 2, C, N])
        masked = sb("masked", [P, 2, HG, C * N])
        wh2 = sb("wh2", [P, C])
        g_max, g_nmax = sb("g_max", [P, C]), sb("g_nmax", [P, C])
        g_sum, g_rec = sb("g_sum", [P, C]), sb("g_rec", [P, C])
        norm = [sb(f"norm{n}", [P, C, D]) for n in range(4)]
        res = [norm[0], sb("res1", [P, C, D]), norm[2], norm[3]]
        stats = [sb(f"stats{n}", [P, C, 6]) for n in range(4)]
        meanvar = [sb(f"meanvar{n}", [P, C, 2]) for n in range(4)]
        vareps = [sb(f"vareps{n}", [P, C]) for n in range(4)]
        rstd = [sb(f"rstd{n}", [P, C]) for n in range(4)]
        hT_full = sb("hT_full", [P, C, N])
        ao_ctx = ExitStack()
        ao = pair("ao", [P, C, N], ao_ctx)
        ao_ctx.close()
        hT = [pair(f"hT{n}", [P, C, N]) for n in (2, 0, 1)]
        hT = [hT[1], hT[2], hT[0]]
        hid_full = sb("hid_full", [P, 2, 2, N])
        hid = pair("hid", [P, UC, N])
        adj1_in = sb("adj1_in", [P, C, N], i32)
        is_rel = sb("is_rel", [P, R, C * N], bf16)
        v_sb = sb("v_sb", [P, C, R * D])
        adj_top, adj_reaches = sb("adj_top", [P, 1]), sb("adj_reaches", [P, 1])
        adj_any, more_flag = sb("adj_any", [P, 1]), sb("more_flag", [P, 1], i32)
        s_max, s_nmax = sb("s_max", [P, 2 * HG * C]), sb("s_nmax", [P, 2 * HG * C])
        s_sum, s_rec = sb("s_sum", [P, 2 * HG * C]), sb("s_rec", [P, 2 * HG * C])

        ps0 = ps("ps0", [P, 3, 512])
        ps_ao = ps("ps_ao", [P, 1, 512])
        ps1 = ps("ps1", [P, 4, 512])

        params_in = event("params_in", 0)
        prep_v = event("prep_v", 0)
        prep_p = event("prep_p", 0)
        gate_v = event("gate_v", 0)
        xT_loaded, x_loaded = event("xT_loaded", 16), event("x_loaded", 16)
        adj0_loaded, adj1_loaded = event("adj0_loaded", 16), event("adj1_loaded", 16)
        x_hi, x_lo = event("x_hi", 1), event("x_lo", 1)
        fence_set = event("fence_set", 1)
        wh_done = event("wh_done", 6)
        wh2_set = event("wh2_set", 2)
        pre_set = event("pre_set", 4)
        score_set = event("score_set", 2)
        g_max_set = event("g_max_set", 4)
        g_nmax_set = event("g_nmax_set", 2)
        att_set = event("att_set", 4)
        g_rec_set = event("g_rec_set", 2)
        whs_hi, whs_lo = event("whs_hi", 4), event("whs_lo", 4)
        att_hi, att_lo = event("att_hi", 2), event("att_lo", 2)
        mix_done = event("mix_done", 2)
        h1_hi, h1_lo = event("h1_hi", 1), event("h1_lo", 1)
        ysum = [event(f"ysum{n}", 1) for n in range(4)]
        stat_set = [event(f"stat_set{n}", 2) for n in range(4)]
        mv_set = [event(f"mv_set{n}", 2) for n in range(4)]
        ve_set = [event(f"ve_set{n}", 1) for n in range(4)]
        rstd_set = [event(f"rstd_set{n}", 1) for n in range(4)]
        norm_set = [event(f"norm_set{n}", 2) for n in range(4)]
        res_set = [event(f"res_set{n}", 2) for n in range(4)]
        turned = [event(f"turned{n}", 1) for n in range(3)]
        hT_set = [event(f"hT_set{n}", 2) for n in range(3)]
        hT_hi = [event(f"hT_hi{n}", 1) for n in range(3)]
        hT_lo = [event(f"hT_lo{n}", 1) for n in range(3)]
        up_done = [event(f"up_done{l}", UC // 2) for l in range(2)]
        hid_set = [event(f"hid_set{l}", UC) for l in range(2)]
        hid_hi = [event(f"hid_hi{l}", UC // 2) for l in range(2)]
        hid_lo = [event(f"hid_lo{l}", UC // 2) for l in range(2)]
        down_done = [event(f"down_done{l}", 1) for l in range(2)]
        rel_set, rel_more_set = event("rel_set", RA), event("rel_more_set", R - RA)
        adj_top_set, adj_reaches_set = event("adj_top_set", 1), event("adj_reaches_set", 1)
        adj_any_set, flag_set = event("adj_any_set", 1), event("flag_set", 1)
        gate_p, gate_t = event("gate_p", 0), event("gate_t", 0)
        qk_done, qk_set = event("qk_done", 2), event("qk_set", 4)
        v_done, v_set = event("v_done", 2), event("v_set", 2)
        v_more_done, v_more_set = event("v_more_done", 2), event("v_more_set", 2)
        s_done = event("s_done", HG)
        s_max_set, s_nmax_set = event("s_max_set", 4), event("s_nmax_set", 4)
        prob_set = event("prob_set", 4 * HG)
        s_rec_set = event("s_rec_set", 4)
        prob_scaled = event("prob_scaled", 4)
        prob_turned = event("prob_turned", 2 * HG)
        probT_set = event("probT_set", 2 * HG)
        masked_set, masked_more_set = event("masked_set", 4 * RA), event("masked_more_set", 4 * (R - RA))
        av_done, av_more_done = event("av_done", 2 * RA), event("av_more_done", 2 * (R - RA))
        ao_hi, ao_lo = event("ao_hi", 2), event("ao_lo", 2)
        wo_done = event("wo_done", 1)
        stored = event("stored", 16)

        def chunk(t, c):
            return t[:, c, :]

        def relations_of(t):
            return not isinstance(t, int) or -1 <= t < B - 1

        def sp_body(sp, t, gat, att1):
            if gat:
                c = t + 2
                if not isinstance(t, int) or c > 0:
                    sp.wait_ge(*x_lo(c - 1, 1))
                sp.dma_start(xT_in[:], xT[c].rearrange("(k p) n -> p k n", p=P)).then_inc(xT_loaded.sem, 16)
                if not isinstance(t, int) or c > 0:
                    sp.wait_ge(*g_max_set(c - 1, 4))
                sp.dma_start(adj0_in[:], adjT[c].rearrange("(k p) n -> p k n", p=P)).then_inc(adj0_loaded.sem, 16)
                if not isinstance(t, int) or c > 0:
                    sp.wait_ge(*ysum[0](c - 1, 1))
                sp.dma_start(x_in[:], x[c].rearrange("(k p) n -> p k n", p=P)).then_inc(x_loaded.sem, 16)
            if not isinstance(t, int) or -1 <= t < B - 1:
                if not isinstance(t, int) or t >= 0:
                    sp.wait_ge(*rel_set(t, RA))
                    sp.wait_ge(*rel_more_set(t, R - RA))
                sp.dma_start(adj1_in[:], adjT[t + 1].rearrange("(k p) n -> p k n", p=P)).then_inc(adj1_loaded.sem, 16)
            if att1:
                sp.wait_ge(*res_set[3](t, 2))
                sp.dma_start(out[t].rearrange("(k p) n -> p k n", p=P), norm[3][:]).then_inc(stored.sem, 16)

        def product(ps_out, left, right, first, last):
            nc.tensor.matmul(ps_out, left[0], right[0], start=first, stop=False)
            nc.tensor.matmul(ps_out, left[0], right[1], start=False, stop=False)
            return nc.tensor.matmul(ps_out, left[1], right[0], start=False, stop=last)

        more = {}

        def cut(halves, *index):
            return tuple(h[(slice(None), *index)] for h in halves)

        def nodes(c):
            return slice(c * P, (c + 1) * P)

        def pe_gat_wh1(pe, g, l):
            if l == 0:
                pe.wait_ge(*x_hi(g, 1))
                pe.wait_ge(*x_lo(g, 1))
                if not isinstance(g, int) or g > 0:
                    pe.wait_ge(*hT_set[1](g - 1, 2))
            else:
                pe.wait_ge(*h1_hi(g, 1))
                pe.wait_ge(*h1_lo(g, 1))
            for k in range(C):
                last = product(ps0[:, 2, 0:N], cut(gat_a[l], k), cut(gT, k), k == 0, k == C - 1)
            last.then_inc(wh_done.sem, 1)

        def pe_gat_wh(pe, g, l, i):
            for k in range(C):
                last = product(ps0[:, i, 0:WE], cut(gT, k, nodes(i)), cut(gat_w[l], k), k == 0, k == C - 1)
            last.then_inc(wh_done.sem, 1)

        def pe_gat_mix(pe, g, l):
            pe.wait_ge(*whs_lo(g, 2 * l + 2))
            pe.wait_ge(*att_lo(g, l + 1))
            left, right = (wh_s, att_s) if l == 0 else (att_s, wh_s)
            for i in range(C):
                for k in range(C):
                    last = product(ps0[:, 2, i * 256:(i + 1) * 256], cut(left, k, nodes(i)), cut(right, k),
                                   k == 0, k == C - 1)
            last.then_inc(mix_done.sem, 1)

        def pe_turn(pe, g, n, bank):
            pe.wait_ge(*norm_set[n](g, 2))
            for i in range(C):
                for f in range(C):
                    last = nc.tensor.transpose(bank[:, f * N + i * P:f * N + (i + 1) * P],
                                               norm[n][:, i, nodes(f)], ident[:])
            last.then_inc(turned[n].sem, 1)

        ff_in = [0, 2]
        ff_bank = [[ps0[:, m, :] for m in (0, 1, 2, 0)], [ps1[:, m, :] for m in (3, 2, 1, 0)]]
        ff_out = [ps0[:, 1, :], ps1[:, 3, :]]

        def pe_up(pe, g, l, m):
            for _ in range(1):
                if m == 0:
                    pe.wait_ge(*hT_hi[ff_in[l]](g, 1))
                    pe.wait_ge(*hT_lo[ff_in[l]](g, 1))
                if m == 3 and l == 0:
                    pe.wait_ge(*hid_set[l](g, 2))
                for u in range(2):
                    for k in range(C):
                        last = product(ff_bank[l][m][:, u * N:(u + 1) * N], cut(up_w[l], k, nodes(2 * m + u)),
                                       cut(hT[ff_in[l]], k), k == 0, k == C - 1)
                last.then_inc(up_done[l].sem, 1)

        def pe_down(pe, g, l, i, half):
            if i == 0 and half == 0 and l == 0:
                pe.wait_ge(*hid_set[0](g, 4))
            for k in range(half * UC // 2, (half + 1) * UC // 2):
                if i == 0 and k % 2 == 0:
                    pe.wait_ge(*hid_lo[l](g, k // 2 + 1))
                last = product(ff_out[l][:, i * D:(i + 1) * D], cut(hid, k, nodes(i)), cut(down_w[l], k),
                               k == 0, k == UC - 1)
            if i == C - 1 and half == 1:
                last.then_inc(down_done[l].sem, 1)

        def pe_qk(pe, g):
            pe.wait_ge(*hT_hi[1](g, 1))
            pe.wait_ge(*hT_lo[1](g, 1))
            for b, w in enumerate((q_w, k_w)):
                for c in range(C):
                    for k in range(C):
                        last = product(ps1[:, b, c * N:(c + 1) * N], cut(w, k, nodes(c)), cut(hT[1], k),
                                       k == 0, k == C - 1)
                last.then_inc(qk_done.sem, 1)

        V_PARTS = [(0, 0), (1, 0), (0, 1), (1, 1)]

        def v_product(g, n):
            j, rr = V_PARTS[n]
            for k in range(C):
                last = product(ps_ao[:, 0, :], cut(hT[1], k, nodes(j)), cut(v_w, k, slice(rr * 512, rr * 512 + 512)),
                               k == 0, k == C - 1)
            return last

        def pe_v(pe, g, n):
            if n:
                pe.wait_ge(*v_set(g, n))
            v_product(g, n).then_inc(v_done.sem, 1)

        def pe_flag(pe, g):
            pe.wait_ge(*flag_set(g, 1))
            pe.sem_inc(gate_t.sem, 1)
            more["pe"] = pe.value_load(more_flag[0:1, 0:1])

        def pe_v_more(pe, g):
            with pe.If(more["pe"] > 0):
                for n in range(2):
                    pe.wait_ge(*(v_more_set(g, 1) if n else v_set(g, 2)))
                    v_product(g, 2 + n).then_inc(v_more_done.sem, 1)
            with pe.Else():
                pe.sem_inc(v_more_done.sem, 2)

        def pe_scores(pe, g, hg, m):
            heads = (2 * m, 2 * m + 1)
            for h in heads:
                if hg == 0 and h == 0:
                    pe.wait_ge(*qk_set(g, 4))
                if hg == 0 and h == 3 and (not isinstance(g, int) or g > 0):
                    pe.wait_ge(*ysum[3](g - 1, 1))
                if hg == 1:
                    pe.wait_ge(*probT_set(g, h + 1))
            for i in range(C):
                for h in heads:
                    rows = slice(h * DH, (h + 1) * DH)
                    last = nc.tensor.matmul(ps1[:, h, i * N:(i + 1) * N], qk[rows, 0, hg, nodes(i)],
                                            qk[rows, 1, hg, :], start=True, stop=True)
            last.then_inc(s_done.sem, 1)

        def pe_prob_turn(pe, g, hg, m):
            for h in (2 * m, 2 * m + 1):
                if h % 2 == 0:
                    pe.wait_ge(*prob_scaled(g, 2 * hg + h // 2 + 1))
                for i in range(C):
                    for j in range(C):
                        last = nc.tensor.transpose(ps1[:, h, j * N + i * P:j * N + (i + 1) * P],
                                                   prob[hg][:, h, i, nodes(j)], ident[:])
                last.then_inc(prob_turned.sem, 1)

        def av_product(hg, r):
            for j in range(C):
                for h in range(HG):
                    col = r * D + hg * P + h * DH
                    last = nc.tensor.matmul(ps_ao[h * DH:(h + 1) * DH, 0, hg * N:(hg + 1) * N],
                                            v_sb[:, j, col:col + DH],
                                            masked[:, r % 2, h, j * N:(j + 1) * N],
                                            start=(r == 0 and j == 0), stop=(r % RA == RA - 1 and j == C - 1),
                                            skip_group_check=True)
            return last

        def pe_av(pe, g, hg, r):
            if r == 0 and hg == 0:
                pe.wait_ge(*v_set(g, 2))
                pe.wait_ge(*v_more_set(g, 2))
            if r == 0 and hg == 1:
                pe.wait_ge(*ao_lo(g, 1))
            pe.wait_ge(*masked_set(g, 2 * (hg * RA + r) + 2))
            av_product(hg, r).then_inc(av_done.sem, 1)

        def pe_av_more(pe, g, hg):
            with pe.If(more["pe"] > 0):
                for r in range(RA, R):
                    pe.wait_ge(*masked_more_set(g, 2 * (hg * (R - RA) + r - RA) + 2))
                    av_product(hg, r).then_inc(av_more_done.sem, 1)
            with pe.Else():
                pe.sem_inc(av_more_done.sem, R - RA)

        def pe_wo(pe, g):
            pe.wait_ge(*ao_lo(g, 2))
            for i in range(C):
                for k in range(C):
                    last = product(ps1[:, 0, i * D:(i + 1) * D], cut(ao, k, nodes(i)), cut(o_w, k), k == 0, k == C - 1)
            last.then_inc(wo_done.sem, 1)

        def pe_body(pe, t, gat, ff0, att1):
            a, b, c = t + 1, t, t + 2
            if att1:
                pe_flag(pe, b)
                pe_qk(pe, b)
                pe_v(pe, b, 0)
            if ff0:
                pe_up(pe, a, 0, 0)
            if att1:
                pe_scores(pe, b, 0, 0)
                pe_scores(pe, b, 0, 1)
            if ff0:
                pe_up(pe, a, 0, 1)
            if att1:
                pe_v(pe, b, 1)
            if ff0:
                pe_up(pe, a, 0, 2)
            if att1:
                pe_v_more(pe, b)
            if ff0:
                pe_up(pe, a, 0, 3)
            if att1:
                pe_prob_turn(pe, b, 0, 0)
                pe_prob_turn(pe, b, 0, 1)
            if ff0:
                pe_down(pe, a, 0, 0, 0)
            if att1:
                pe_scores(pe, b, 1, 0)
            if ff0:
                pe_down(pe, a, 0, 0, 1)
            if att1:
                pe_scores(pe, b, 1, 1)
                pe_av(pe, b, 0, 0)
            if ff0:
                pe_down(pe, a, 0, 1, 0)
            if att1:
                pe_av(pe, b, 0, 1)
            if ff0:
                pe_down(pe, a, 0, 1, 1)
            if att1:
                pe_av_more(pe, b, 0)
                pe_prob_turn(pe, b, 1, 0)
                pe_prob_turn(pe, b, 1, 1)
            if ff0:
                pe_turn(pe, a, 1, ps0[:, 2, :])
            if gat:
                pe_gat_wh1(pe, c, 0)
            if att1:
                pe_av(pe, b, 1, 0)
            if gat:
                pe_gat_wh(pe, c, 0, 1)
                pe_gat_wh(pe, c, 0, 0)
            if att1:
                pe_av(pe, b, 1, 1)
                pe_av_more(pe, b, 1)
                pe_wo(pe, b)
            if gat:
                pe_gat_mix(pe, c, 0)
            if att1:
                pe_turn(pe, b, 2, ps1[:, 1, :])
            if gat:
                pe_gat_wh1(pe, c, 1)
                pe_gat_wh(pe, c, 1, 0)
                pe_gat_wh(pe, c, 1, 1)
            if att1:
                pe_up(pe, b, 1, 0)
                pe_up(pe, b, 1, 1)
                pe_up(pe, b, 1, 2)
                pe_up(pe, b, 1, 3)
            if gat:
                pe_gat_mix(pe, c, 1)
            if att1:
                pe_down(pe, b, 1, 0, 0)
                pe_down(pe, b, 1, 0, 1)
                pe_down(pe, b, 1, 1, 0)
            if gat:
                pe_turn(pe, c, 0, ps0[:, 0, :])
            if att1:
                pe_down(pe, b, 1, 1, 1)

        def act_gat_pre(act, g, l):
            act.wait_ge(*wh_done(g, 3 * l + 3))
            act.wait_ge(*wh2_set(g, l + 1))
            for j in range(C):
                act.activation(score[:, j, :], ps0[:, 2, 0:N], ACT.Identity, bias=wh2[:, j:j + 1]).then_inc(pre_set.sem, 1)

        def act_gat_exp(act, g, l):
            act.wait_ge(*g_nmax_set(g, l + 1))
            for j in range(C):
                act.activation(score[:, j, :], score[:, j, :], ACT.Exp, bias=g_nmax[:, j:j + 1],
                               accum_out=g_sum[:, j:j + 1]).then_inc(att_set.sem, 1)

        def act_h1(act, g):
            act.wait_ge(*mix_done(g, 1))
            act.activation(gT[0][:].rearrange("p c n -> p (c n)"), ps0[:, 2, :], ACT.Copy).then_inc(h1_hi.sem, 1)

        def act_turned(act, g, n, bank):
            act.wait_ge(*turned[n](g, 1))
            for f in range(C):
                act.activation(hT_full[:, f, :], bank[:, f * N:(f + 1) * N], ACT.Identity,
                               bias=shift_col[n][:, f:f + 1], scale=gain_col[n][:, f:f + 1]).then_inc(hT_set[n].sem, 1)
            act.wait_ge(*hT_set[n](g, 2))
            act.activation(hT[n][0][:], hT_full[:], ACT.Copy).then_inc(hT_hi[n].sem, 1)

        def act_hidden(act, g, l, m):
            for _ in range(1):
                act.wait_ge(*up_done[l](g, m + 1))
                if m >= 2:
                    act.wait_ge(*hid_lo[l](g, m - 1))
                for u in range(2):
                    act.activation(hid_full[:, m % 2, u, :], ff_bank[l][m][:, u * N:(u + 1) * N],
                                   ACT.Relu if l == 0 else ACT.Gelu,
                                   bias=up_bias[l][:, 2 * m + u:2 * m + u + 1]).then_inc(hid_set[l].sem, 1)
                act.wait_ge(*hid_set[l](g, 2 * m + 2))
                act.activation(hid[0][:, 2 * m:2 * m + 2, :], hid_full[:, m % 2, :, :], ACT.Copy).then_inc(hid_hi[l].sem, 1)

        def act_qk(act, g):
            for b in range(2):
                act.wait_ge(*qk_done(g, b + 1))
                for c in range(C):
                    act.activation(qk[:, b, c, :], ps1[:, b, c * N:(c + 1) * N], ACT.Identity,
                                   bias=qk_bias[:, b, c:c + 1]).then_inc(qk_set.sem, 1)

        def act_prob(act, g, hg, m):
            for h in (2 * m, 2 * m + 1):
                if h % 2 == 0:
                    act.wait_ge(*s_nmax_set(g, 2 * hg + h // 2 + 1))
                for i in range(C):
                    col = (hg * HG + h) * C + i
                    act.activation(prob[hg][:, h, i, :], ps1[:, h, i * N:(i + 1) * N], ACT.Exp,
                                   bias=s_nmax[:, col:col + 1], scale=SCALE,
                                   accum_out=s_sum[:, col:col + 1]).then_inc(prob_set.sem, 1)

        def act_prob_turned(act, g, hg, m):
            for h in (2 * m, 2 * m + 1):
                act.wait_ge(*prob_turned(g, hg * HG + h + 1))
                act.activation(prob[hg][:, h, :, :].rearrange("p c n -> p (c n)"), ps1[:, h, :],
                               ACT.Copy).then_inc(probT_set.sem, 1)

        def act_ao(act, g, hg):
            act.wait_ge(*av_done(g, (hg + 1) * RA))
            act.wait_ge(*av_more_done(g, (hg + 1) * (R - RA)))
            act.activation(ao[0][:, hg, :], ps_ao[:, 0, hg * N:(hg + 1) * N], ACT.Copy).then_inc(ao_hi.sem, 1)

        def act_body(act, t, gat, ff0, att1):
            a, b, c = t + 1, t, t + 2
            if att1:
                act_qk(act, b)
            if ff0:
                act_hidden(act, a, 0, 0)
            if att1:
                act_prob(act, b, 0, 0)
                act_prob(act, b, 0, 1)
            if ff0:
                act_hidden(act, a, 0, 1)
                act_hidden(act, a, 0, 2)
                act_hidden(act, a, 0, 3)
            if att1:
                act_prob_turned(act, b, 0, 0)
                act_prob_turned(act, b, 0, 1)
                act_prob(act, b, 1, 0)
                act_prob(act, b, 1, 1)
                act_ao(act, b, 0)
                act_prob_turned(act, b, 1, 0)
                act_prob_turned(act, b, 1, 1)
            if ff0:
                act_turned(act, a, 1, ps0[:, 2, :])
            if gat:
                act_gat_pre(act, c, 0)
                act_gat_exp(act, c, 0)
            if att1:
                act_ao(act, b, 1)
            if gat:
                act_h1(act, c)
            if att1:
                act_turned(act, b, 2, ps1[:, 1, :])
            if gat:
                act_gat_pre(act, c, 1)
                act_gat_exp(act, c, 1)
            if att1:
                act_hidden(act, b, 1, 0)
                act_hidden(act, b, 1, 1)
                act_hidden(act, b, 1, 2)
                act_hidden(act, b, 1, 3)
            if gat:
                act_turned(act, c, 0, ps0[:, 0, :])

        def dve_gat_in(dve, g):
            dve.wait_ge(*xT_loaded(g, 16))
            dve.tensor_copy(gT[0][:], xT_in[:]).then_inc(x_hi.sem, 1)

        def dve_fence(dve, g):
            dve.wait_ge(*adj0_loaded(g, 16))
            dve.tensor_scalar(fence, adj0_in[:], 0.0, NEG, ALU.is_le, ALU.mult).then_inc(fence_set.sem, 1)

        def dve_gat_wh2(dve, g, l):
            dve.wait_ge(*wh_done(g, 3 * l + 3))
            dve.tensor_copy(wh2[:].unsqueeze(2), ps0[:, 0:C, D:D + 1]).then_inc(wh2_set.sem, 1)

        def dve_gat_score(dve, g, l):
            dve.wait_ge(*pre_set(g, 2 * l + 2))
            dve.scalar_tensor_tensor(out=score[:], in0=score[:], scalar=ALPHA, in1=score[:],
                                     op0=ALU.mult, op1=ALU.max).then_inc(score_set.sem, 1)
            dve.wait_ge(*score_set(g, l + 1))
            if l == 0:
                dve.wait_ge(*fence_set(g, 1))
            dve.sem_inc(gate_v.sem, 1)
            for j in range(C):
                dve.tensor_tensor_reduce(out=score[:, j, :], in0=score[:, j, :], in1=fence[:, j, :], scale=1.0,
                                         scalar=-3.0e38, op0=ALU.add, op1=ALU.max,
                                         accum_out=g_max[:, j:j + 1]).then_inc(g_max_set.sem, 1)
            dve.wait_ge(*g_max_set(g, 2 * l + 2))
            dve.tensor_scalar(g_nmax[:], g_max[:], -1.0, None, ALU.mult).then_inc(g_nmax_set.sem, 1)

        def dve_gat_split(dve, g, l):
            dve.wait_ge(*att_set(g, 2 * l + 2))
            dve.reciprocal(g_rec[:], g_sum[:]).then_inc(g_rec_set.sem, 1)
            dve.tensor_copy(att_s[0][:], score[:]).then_inc(att_hi.sem, 1)
            dve.wait_ge(*g_rec_set(g, l + 1))
            for j in range(C):
                dve.tensor_scalar(wh_s[0][:, j, :], ps0[:, j, 0:D], g_rec[:, j:j + 1], None,
                                  ALU.mult).then_inc(whs_hi.sem, 1)
            dve.wait_ge(*att_hi(g, l + 1))
            dve.tensor_tensor(att_s[1][:], score[:], value(att_s[0][:]), ALU.subtract).then_inc(att_lo.sem, 1)
            dve.wait_ge(*whs_hi(g, 2 * l + 2))
            for j in range(C):
                dve.scalar_tensor_tensor(out=wh_s[1][:, j, :], in0=ps0[:, j, 0:D], scalar=g_rec[:, j:j + 1],
                                         in1=value(wh_s[0][:, j, :]), op0=ALU.mult,
                                         op1=ALU.subtract).then_inc(whs_lo.sem, 1)

        def dve_h1(dve, g):
            dve.wait_ge(*h1_hi(g, 1))
            dve.tensor_tensor(gT[1][:].rearrange("p c n -> p (c n)"), ps0[:, 2, :],
                              value(gT[0][:]).rearrange("p c n -> p (c n)"), ALU.subtract).then_inc(h1_lo.sem, 1)

        ln_bank = [ps0[:, 2, :], ff_out[0], ps1[:, 0, :], ff_out[1]]
        ln_done = [lambda g: mix_done(g, 2), lambda g: down_done[0](g, 1), lambda g: wo_done(g, 1),
                   lambda g: down_done[1](g, 1)]

        def dve_norm(dve, g, n):
            dve.wait_ge(*ln_done[n](g))
            dve.wait_ge(*(x_loaded(g, 16) if n == 0 else res_set[n - 1](g, 2)))
            if n == 3 and (not isinstance(g, int) or g > 0):
                dve.wait_ge(*stored(g - 1, 16))
            residual = x_in if n == 0 else res[n - 1]
            y = norm[n]
            dve.tensor_tensor(y[:].rearrange("p c n -> p (c n)"), ln_bank[n],
                              residual[:].rearrange("p c n -> p (c n)"), ALU.add).then_inc(ysum[n].sem, 1)
            dve.wait_ge(*ysum[n](g, 1))
            for i in range(C):
                dve.bn_stats(stats[n][:, i, :], y[:, i, :]).then_inc(stat_set[n].sem, 1)
            dve.wait_ge(*stat_set[n](g, 2))
            dve.sem_inc(gate_v.sem, 1)
            for i in range(C):
                dve.bn_aggr(meanvar[n][:, i, :], stats[n][:, i, :]).then_inc(mv_set[n].sem, 1)
            dve.wait_ge(*mv_set[n](g, 2))
            dve.tensor_scalar(vareps[n][:].unsqueeze(2), meanvar[n][:, :, 1:2], EPS, None, ALU.add).then_inc(ve_set[n].sem, 1)

        def dve_norm_end(dve, g, n):
            dve.wait_ge(*rstd_set[n](g, 1))
            for i in range(C):
                dve.tensor_scalar(norm[n][:, i, :], norm[n][:, i, :], meanvar[n][:, i, 0:1], rstd[n][:, i:i + 1],
                                  ALU.subtract, ALU.mult).then_inc(norm_set[n].sem, 1)

        def dve_adj_top(dve, g):
            dve.wait_ge(*adj1_loaded(g, 16))
            dve.tensor_reduce(adj_top[:], adj1_in[:], AX.XY, ALU.max).then_inc(adj_top_set.sem, 1)
            dve.wait_ge(*adj_top_set(g, 1))
            dve.tensor_scalar(adj_reaches[:], adj_top[:], float(RA), None, ALU.is_ge).then_inc(adj_reaches_set.sem, 1)

        def relation_mask(r):
            return nc.vector.tensor_scalar(is_rel[:, r, :], adj1_in[:].rearrange("p c n -> p (c n)"), float(r), None,
                                           ALU.is_equal)

        def dve_relations(dve, g):
            for r in range(RA):
                relation_mask(r).then_inc(rel_set.sem, 1)

        def dve_relations_more(dve, g):
            dve.wait_ge(*flag_set(g, 1))
            dve.sem_inc(gate_v.sem, 1)
            more["next"] = dve.value_load(more_flag[0:1, 0:1])
            with dve.If(more["next"] > 0):
                for r in range(RA, R):
                    relation_mask(r).then_inc(rel_more_set.sem, 1)
            with dve.Else():
                dve.sem_inc(rel_more_set.sem, R - RA)

        def dve_flag(dve, g):
            dve.wait_ge(*flag_set(g, 1))
            dve.sem_inc(gate_v.sem, 1)
            more["dve"] = dve.value_load(more_flag[0:1, 0:1])

        def v_out(n):
            j, rr = V_PARTS[n]
            return nc.vector.tensor_tensor(v_sb[:, j, rr * 512:(rr + 1) * 512], ps_ao[:, 0, :],
                                           v_bias[:, rr * 512:(rr + 1) * 512], ALU.add)

        def dve_v(dve, g, n):
            dve.wait_ge(*v_done(g, n + 1))
            v_out(n).then_inc(v_set.sem, 1)

        def dve_v_more(dve, g):
            with dve.If(more["dve"] > 0):
                for n in range(2):
                    dve.wait_ge(*v_more_done(g, n + 1))
                    v_out(2 + n).then_inc(v_more_set.sem, 1)
            with dve.Else():
                dve.sem_inc(v_more_set.sem, 2)

        def dve_max(dve, g, hg, m):
            cols = slice((hg * HG + 2 * m) * C, (hg * HG + 2 * m + 2) * C)
            k = 2 * hg + m + 1
            dve.wait_ge(*s_done(g, k))
            dve.tensor_reduce(s_max[:, cols], ps1[:, 2 * m:2 * m + 2, :].rearrange("p b (c n) -> p (b c) n", n=N),
                              AX.X, ALU.max).then_inc(s_max_set.sem, 1)
            dve.wait_ge(*s_max_set(g, k))
            dve.tensor_scalar(s_nmax[:, cols], s_max[:, cols], -SCALE, None, ALU.mult).then_inc(s_nmax_set.sem, 1)

        def dve_rec(dve, g, hg, m):
            cols = slice((hg * HG + 2 * m) * C, (hg * HG + 2 * m + 2) * C)
            dve.wait_ge(*prob_set(g, C * (hg * HG + 2 * m + 2)))
            dve.reciprocal(s_rec[:, cols], s_sum[:, cols]).then_inc(s_rec_set.sem, 1)

        def mask_pair(hg, r, m):
            return nc.vector.tensor_tensor(masked[:, r % 2, 2 * m:2 * m + 2, :],
                                           prob[hg][:, 2 * m:2 * m + 2, :, :].rearrange("p h c n -> p h (c n)"),
                                           is_rel[:, r:r + 1, :].broadcast_to([P, 2, C * N]), ALU.mult)

        def dve_mask(dve, g, hg, r):
            if r == 0 and hg == 0:
                dve.wait_ge(*rel_set(g, RA))
            if hg == 1:
                dve.wait_ge(*av_done(g, r + 1))
                dve.wait_ge(*av_more_done(g, r + 1))
            for m in range(2):
                if r == 0:
                    dve.wait_ge(*probT_set(g, hg * HG + 2 * m + 2))
                mask_pair(hg, r, m).then_inc(masked_set.sem, 1)

        def dve_mask_more(dve, g, hg):
            with dve.If(more["dve"] > 0):
                dve.wait_ge(*rel_more_set(g, R - RA))
                for r in range(RA, R):
                    dve.wait_ge(*av_done(g, hg * RA + r - RA + 1))
                    for m in range(2):
                        mask_pair(hg, r, m).then_inc(masked_more_set.sem, 1)
            with dve.Else():
                dve.sem_inc(masked_more_set.sem, 2 * (R - RA))

        def dve_ao(dve, g, hg):
            dve.wait_ge(*ao_hi(g, hg + 1))
            dve.tensor_tensor(ao[1][:, hg, :], ps_ao[:, 0, hg * N:(hg + 1) * N], value(ao[0][:, hg, :]),
                              ALU.subtract).then_inc(ao_lo.sem, 1)

        def dve_body(dve, t, gat, ff0, att1):
            a, b, c = t + 1, t, t + 2
            if att1:
                dve_max(dve, b, 0, 0)
                dve_v(dve, b, 0)
                dve_max(dve, b, 0, 1)
                dve_flag(dve, b)
                dve_v(dve, b, 1)
                dve_rec(dve, b, 0, 0)
                dve_v_more(dve, b)
                dve_rec(dve, b, 0, 1)
                dve_mask(dve, b, 0, 0)
                dve_max(dve, b, 1, 0)
                dve_mask(dve, b, 0, 1)
                dve_max(dve, b, 1, 1)
            if relations_of(t):
                dve_adj_top(dve, t + 1)
            if att1:
                dve_rec(dve, b, 1, 0)
                dve_mask_more(dve, b, 0)
            if gat:
                dve_fence(dve, c)
            if att1:
                dve_rec(dve, b, 1, 1)
                dve_ao(dve, b, 0)
            if ff0:
                dve_norm(dve, a, 1)
                dve_norm_end(dve, a, 1)
            if gat:
                dve_gat_in(dve, c)
            if att1:
                dve_mask(dve, b, 1, 0)
                dve_mask(dve, b, 1, 1)
            if gat:
                dve_gat_wh2(dve, c, 0)
            if att1:
                dve_mask_more(dve, b, 1)
            if gat:
                dve_gat_score(dve, c, 0)
                dve_gat_split(dve, c, 0)
            if att1:
                dve_ao(dve, b, 1)
                dve_norm(dve, b, 2)
            if gat:
                dve_h1(dve, c)
            if att1:
                dve_norm_end(dve, b, 2)
            if gat:
                dve_gat_wh2(dve, c, 1)
                dve_gat_score(dve, c, 1)
            if relations_of(t):
                dve_relations_more(dve, t + 1)
            if gat:
                dve_gat_split(dve, c, 1)
                dve_norm(dve, c, 0)
                dve_norm_end(dve, c, 0)
            if relations_of(t):
                dve_relations(dve, t + 1)
            if att1:
                dve_norm(dve, b, 3)
                dve_norm_end(dve, b, 3)

        def pool_gat_in(pool, g):
            pool.wait_ge(*x_hi(g, 1))
            pool.tensor_tensor(gT[1][:], xT_in[:], value(gT[0][:]), ALU.subtract).then_inc(x_lo.sem, 1)

        def pool_rstd(pool, g, n):
            pool.wait_ge(*ve_set[n](g, 1))
            pool.tensor_tensor(rstd[n][:], vareps[n][:], neg_half[:], ALU.pow).then_inc(rstd_set[n].sem, 1)

        def pool_affine(pool, g, n):
            pool.wait_ge(*norm_set[n](g, 2))
            if n in (0, 2):
                pool.wait_ge(*turned[n](g, 1))
            if n == 1 and (not isinstance(g, int) or g > 0):
                pool.wait_ge(*ysum[2](g - 1, 1))
            pool.tensor_tensor(res[n][:], norm[n][:], gain_row[n][:].unsqueeze(1).broadcast_to([P, C, D]),
                               ALU.mult).then_inc(res_set[n].sem, 1)
            pool.wait_ge(*res_set[n](g, 1))
            pool.tensor_tensor(res[n][:], res[n][:], shift_row[n][:].unsqueeze(1).broadcast_to([P, C, D]),
                               ALU.add).then_inc(res_set[n].sem, 1)

        def pool_hT(pool, g, n):
            pool.wait_ge(*hT_hi[n](g, 1))
            pool.tensor_tensor(hT[n][1][:], hT_full[:], value(hT[n][0][:]), ALU.subtract).then_inc(hT_lo[n].sem, 1)

        def pool_hidden(pool, g, l, m):
            for _ in range(1):
                pool.wait_ge(*hid_hi[l](g, m + 1))
                pool.tensor_tensor(hid[1][:, 2 * m:2 * m + 2, :], hid_full[:, m % 2, :, :],
                                   value(hid[0][:, 2 * m:2 * m + 2, :]), ALU.subtract).then_inc(hid_lo[l].sem, 1)

        def pool_prob(pool, g, hg, m):
            for _ in range(1):
                first = (hg * HG + 2 * m) * C
                pool.wait_ge(*s_rec_set(g, 2 * hg + m + 1))
                part = prob[hg][:, 2 * m:2 * m + 2, :, :].rearrange("p h c n -> p (h c) n")
                pool.tensor_tensor(part, part, s_rec[:, first:first + 2 * C].unsqueeze(2).broadcast_to([P, 2 * C, N]),
                                   ALU.mult).then_inc(prob_scaled.sem, 1)

        def pool_flag(pool, g):
            pool.wait_ge(*adj_reaches_set(g, 1))
            pool.sem_inc(gate_p.sem, 1)
            pool.partition_all_reduce(adj_any[:], adj_reaches[:], P, bass.bass_isa.ReduceOp.max).then_inc(adj_any_set.sem, 1)
            pool.wait_ge(*adj_any_set(g, 1))
            pool.sem_inc(gate_p.sem, 1)
            pool.tensor_copy(more_flag[:], adj_any[:]).then_inc(flag_set.sem, 1)

        def pool_body(pool, t, gat, ff0, att1):
            a, b, c = t + 1, t, t + 2
            if ff0:
                pool_hidden(pool, a, 0, 0)
            if att1:
                pool_prob(pool, b, 0, 0)
            if ff0:
                pool_hidden(pool, a, 0, 1)
            if att1:
                pool_prob(pool, b, 0, 1)
            if ff0:
                pool_hidden(pool, a, 0, 2)
                pool_hidden(pool, a, 0, 3)
            if att1:
                pool_prob(pool, b, 1, 0)
                pool_prob(pool, b, 1, 1)
            if ff0:
                pool_rstd(pool, a, 1)
            if gat:
                pool_gat_in(pool, c)
            if relations_of(t):
                pool_flag(pool, t + 1)
            if ff0:
                pool_hT(pool, a, 1)
            if att1:
                pool_rstd(pool, b, 2)
                pool_hT(pool, b, 2)
            if ff0:
                pool_affine(pool, a, 1)
            if att1:
                pool_affine(pool, b, 2)
                pool_hidden(pool, b, 1, 0)
                pool_hidden(pool, b, 1, 1)
                pool_hidden(pool, b, 1, 2)
            if gat:
                pool_rstd(pool, c, 0)
            if att1:
                pool_hidden(pool, b, 1, 3)
            if gat:
                pool_hT(pool, c, 0)
            if att1:
                pool_rstd(pool, b, 3)
            if gat:
                pool_affine(pool, c, 0)
            if att1:
                pool_affine(pool, b, 3)

        def rows(w):
            return w.rearrange("(k p) n -> p k n", p=P)

        def across(v):
            return v.unsqueeze(0).broadcast_to([P, v.shape[0]])

        loads = [(raw_gat[l][:, :, 0:D], rows(p0[f"W{l + 1}"])) for l in range(2)]
        loads += [(raw_a[l][:], across(p0[f"a{l + 1}"].rearrange("n o -> (n o)"))) for l in range(2)]
        loads += [(raw_up[0][:], rows(p0["w_ff1"])), (raw_down[0][:], rows(p0["w_ff2"]))]
        loads += [(raw_qko[m][:], rows(p1[w])) for m, w in enumerate(("Wq", "Wk", "Wo"))]
        loads += [(raw_v[:, :, r * D:(r + 1) * D], rows(p1["Wv"][r])) for r in range(R)]
        loads += [(v_bias[:, r * D:(r + 1) * D], across(p1["bv"][r])) for r in range(R)]
        loads += [(raw_up[1][:], rows(p1["W1"])), (raw_down[1][:], rows(p1["W2"]))]
        gains = [p0["g_ln1"], p0["g_ln2"], p1["g1"], p1["g2"]]
        shifts = [p0["b_ln1"], p0["b_ln2"], p1["beta1"], p1["beta2"]]
        loads += [(gain_row[n][:], across(gains[n])) for n in range(4)]
        loads += [(shift_row[n][:], across(shifts[n])) for n in range(4)]
        loads += [(raw_next[n][:], across(v)) for n, v in enumerate((p0["b_ff2"], p1["bo"], p1["b2"]))]
        by_feature = [(gain_col[n][:], gains[n]) for n in range(3)] + [(shift_col[n][:], shifts[n]) for n in range(3)]
        by_feature += [(up_bias[0][:], p0["b_ff1"]), (up_bias[1][:], p1["b1"])]
        by_feature += [(qk_bias[:, 0, :], p1["bq"]), (qk_bias[:, 1, :], p1["bk"])]
        ALL_LOADED = 16 * (len(loads) + len(by_feature))

        splits = [(raw_gat[l], gat_w[l]) for l in range(2)] + [(raw_arep[l], gat_a[l]) for l in range(2)]
        splits += [(raw_up[l], up_w[l]) for l in range(2)] + [(raw_down[l], down_w[l]) for l in range(2)]
        splits += [(raw_qko[0], q_w), (raw_qko[1], k_w), (raw_qko[2], o_w), (raw_v, v_w)]
        WA, PLACED = 8, 8 + 6
        HI = PLACED + len(splits)
        PREP_V = HI + len(splits) + 3
        PREP_P = 4

        def sp_setup(sp):
            for dst, src in loads:
                sp.dma_start(dst, src).then_inc(params_in.sem, 16)
            for dst, src in by_feature:
                sp.dma_start(dst, src.rearrange("(c p) -> p c", p=P), allow_slow_non_contiguous=True)\
                  .then_inc(params_in.sem, 16)
            sp.wait_ge(prep_v.sem, PREP_V)

        def dve_setup(dve):
            dve.wait_ge(params_in.sem, ALL_LOADED)
            for l in range(2):
                for half in range(2):
                    for k in range(C):
                        dst = raw_wa[:, l, k:k + 1] if half == 0 else raw_gat[l][:, k, D:D + 1]
                        dve.tensor_tensor_reduce(out=raw_prod[:, l, half, k, :], in0=raw_gat[l][:, k, 0:D],
                                                 in1=raw_a[l][:, half * D:(half + 1) * D], scale=1.0, scalar=0.0,
                                                 op0=ALU.mult, op1=ALU.add, accum_out=dst).then_inc(prep_v.sem, 1)
            for l in range(2):
                dve.memset(raw_gat[l][:, :, D + 1:WE], 0.0).then_inc(prep_v.sem, 1)
            dve.wait_ge(prep_v.sem, WA)
            for l in range(2):
                for k in range(C):
                    dve.tensor_copy(raw_arep[l][:, k, :], raw_wa[:, l, k:k + 1].broadcast_to([P, P])).then_inc(prep_v.sem, 1)
            dve.wait_ge(prep_v.sem, PLACED)
            for raw, (hi, _) in splits:
                dve.tensor_copy(hi[:], raw[:]).then_inc(prep_v.sem, 1)
            dve.wait_ge(prep_v.sem, HI)
            for raw, (hi, lo) in splits:
                dve.tensor_tensor(lo[:], raw[:], value(hi[:]), ALU.subtract).then_inc(prep_v.sem, 1)
            for n in range(3):
                dve.tensor_tensor(shift_row[n][:], shift_row[n][:], raw_next[n][:], ALU.add).then_inc(prep_v.sem, 1)
            dve.wait_ge(prep_v.sem, PREP_V)

        def pool_setup(pool):
            pool.memset(ident[:], 0.0).then_inc(prep_p.sem, 1)
            pool.memset(neg_half[:], -0.5).then_inc(prep_p.sem, 1)
            pool.wait_ge(prep_p.sem, 2)
            pool.affine_select(out=ident[:], in_=ident[:], compare_op=ALU.not_equal, fill=1.0, base=0,
                               pattern=[[-1, P]], channel_multiplier=1).then_inc(prep_p.sem, 2)
            pool.wait_ge(prep_p.sem, PREP_P)
            pool.wait_ge(prep_v.sem, PREP_V)

        def ready(eng):
            eng.wait_ge(prep_v.sem, PREP_V)
            eng.wait_ge(prep_p.sem, PREP_P)

        def run(eng, body):
            body(eng, -2, True, False, False)
            body(eng, -1, True, True, False)
            body(eng, 0, True, True, True)
            with eng.Fori(1, B - 2) as t:
                body(eng, t, True, True, True)
            body(eng, B - 2, False, True, True)
            body(eng, B - 1, False, False, True)

        block = ctx.enter_context(nc.Block())

        @block.sync
        def _(sp):
            sp_setup(sp)
            run(sp, lambda e, t, gat, ff0, att1: sp_body(e, t, gat, att1))
            sp.wait_ge(*stored(B - 1, 16))

        @block.tensor
        def _(pe):
            ready(pe)
            run(pe, pe_body)

        @block.scalar
        def _(act):
            ready(act)
            run(act, act_body)

        @block.vector
        def _(dve):
            dve_setup(dve)
            run(dve, dve_body)

        @block.gpsimd
        def _(pool):
            pool_setup(pool)
            run(pool, pool_body)


_L0 = ["W1", "a1", "W2", "a2", "w_ff1", "b_ff1", "w_ff2", "b_ff2", "g_ln1", "b_ln1", "g_ln2", "b_ln2"]
_L1 = ["Wq", "bq", "Wk", "bk", "Wv", "bv", "Wo", "bo", "W1", "b1", "W2", "b2", "g1", "beta1", "g2", "beta2"]


def kernel(**inputs):
    import numpy as np
    import concourse.bacc as bacc
    from concourse.bass_utils import run_bass_kernel_spmd

    nc = bacc.Bacc("TRN2", target_bir_lowering=False, num_devices=1, dynamic_dma_scratch_size=1024)
    arrays = {}

    def given(name, a):
        a = np.ascontiguousarray(a)
        arrays[name] = a
        return nc.dram_tensor(name, a.shape, mybir.dt.from_np(a.dtype), kind="ExternalInput").ap()

    xs, adj = np.asarray(inputs["x"]), np.asarray(inputs["adj"])
    x = given("x_nodes", xs)
    xT = given("x_features", xs.transpose(0, 2, 1))
    adjT = given("adj_keys", adj.transpose(0, 2, 1))
    p0 = {n: given(f"L0_{n}", inputs[f"L0_gnn_{n}"]) for n in _L0}
    p1 = {n: given(f"L1_{n}", inputs[f"L1_gnn_{n}"]) for n in _L1}
    out = nc.dram_tensor("out_nodes", xs.shape, mybir.dt.float32, kind="ExternalOutput").ap()
    adj_seq_kernel(nc, x, xT, adjT, p0, p1, out)
    r = run_bass_kernel_spmd(nc, [arrays], core_ids=[0])
    return r.results[0]["out_nodes"]
```

```python
import concourse.bass as bass
from concourse import mybir
from contextlib import ExitStack


class Event:

    def __init__(self, sem, per_graph):
        self.sem, self.per_graph = sem, per_graph

    def __call__(self, g, n):
        return self.sem, g * self.per_graph + n


def adj_seq_kernel(nc: bass.Bass, x, xT, adjT, p0, p1, out):
    f32, f32r, i32 = mybir.dt.float32, mybir.dt.float32r, mybir.dt.int32
    ALU, ACT, AX = mybir.AluOpType, mybir.ActivationFunctionType, mybir.AxisListType

    B, N, D = x.shape
    P = 128
    C = D // P
    assert N == D == C * P
    U = p0["w_ff1"].shape[1]
    UC = U // P
    R = p1["Wv"].shape[0]
    RA = 2
    H = 8
    DH = D // H
    HG = P // DH
    SCALE = 1.0 / float(DH) ** 0.5
    ALPHA, NEG, EPS = 0.2, -9000000000000000.0, 1e-5
    WE = D + 2

    ctx = ExitStack()
    with ctx:
        def sb(name, shape, dt=f32, c=ctx):
            return c.enter_context(nc.sbuf_tensor(name, shape, dt))

        def pair(name, shape, c=ctx):
            return sb(name + "_hi", shape, f32r, c), sb(name + "_lo", shape, f32r, c)

        def staged_pair(name, full_name, shape):
            hi, first = sb(name + "_hi", shape, f32r), ExitStack()
            full = sb(full_name, shape, f32, first)
            first.close()
            return (hi, sb(name + "_lo", shape, f32r)), full

        def ps(name, shape):
            return ctx.enter_context(nc.psum_tensor(name, shape, f32))

        def event(name, per_graph):
            return Event(ctx.enter_context(nc.semaphore(name)), per_graph)

        def value(t):
            return (t if isinstance(t, bass.AP) else t[:]).bitcast(f32)

        gat_w = [pair(f"gat_w{l}", [P, C, WE]) for l in range(2)]
        gat_a = [pair(f"gat_a{l}", [P, C, P]) for l in range(2)]
        up_w = [pair(f"up_w{l}", [P, C, U]) for l in range(2)]
        down_w = [pair(f"down_w{l}", [P, UC, D]) for l in range(2)]
        q_w, k_w, o_w = pair("q_w", [P, C, D]), pair("k_w", [P, C, D]), pair("o_w", [P, C, D])
        v_w = pair("v_w", [P, C, R * D])
        v_bias = sb("v_bias", [P, R * D])
        gain_row = [sb(f"gain_row{n}", [P, D]) for n in range(4)]
        shift_row = [sb(f"shift_row{n}", [P, D]) for n in range(4)]
        gain_col = [sb(f"gain_col{n}", [P, C]) for n in range(3)]
        shift_col = [sb(f"shift_col{n}", [P, C]) for n in range(3)]
        up_bias = [sb(f"up_bias{l}", [P, UC]) for l in range(2)]
        qk_bias = sb("qk_bias", [P, 2, C])
        ident = sb("ident", [P, P])
        neg_half = sb("neg_half", [P, C])

        raw_ctx = ExitStack()
        raw_gat = [sb(f"raw_gat{l}", [P, C, WE], c=raw_ctx) for l in range(2)]
        raw_a = [sb(f"raw_a{l}", [P, 2 * D], c=raw_ctx) for l in range(2)]
        raw_arep = [sb(f"raw_arep{l}", [P, C, P], c=raw_ctx) for l in range(2)]
        raw_prod = sb("raw_prod", [P, 2, 2, C, D], c=raw_ctx)
        raw_wa = sb("raw_wa", [P, 2, C], c=raw_ctx)
        raw_up = [sb(f"raw_up{l}", [P, C, U], c=raw_ctx) for l in range(2)]
        raw_down = [sb(f"raw_down{l}", [P, UC, D], c=raw_ctx) for l in range(2)]
        raw_qko = [sb(f"raw_{n}", [P, C, D], c=raw_ctx) for n in "qko"]
        raw_v = sb("raw_v", [P, C, R * D], c=raw_ctx)
        raw_next = [sb(f"raw_next{n}", [P, D], c=raw_ctx) for n in range(3)]
        raw_ctx.close()

        adj0_in = sb("adj0_in", [P, C, N], i32)
        fence = value(adj0_in)
        gT, xT_in = staged_pair("gT", "xT_in", [P, C, N])
        att_s, score = staged_pair("att_s", "score", [P, C, N])
        wh_s = pair("wh_s", [P, C, D])
        prob = [sb(f"prob{hg}", [P, HG, C, N]) for hg in range(2)]
        qk = sb("qk", [P, 2, C, N])
        masked = sb("masked", [P, 2, HG, C * N])
        wh2 = sb("wh2", [P, C])
        g_max, g_nmax = sb("g_max", [P, C]), sb("g_nmax", [P, C])
        g_sum, g_rec = sb("g_sum", [P, C]), sb("g_rec", [P, C])
        norm = [sb(f"norm{n}", [P, C, D]) for n in range(4)]
        res = [sb("res0", [P, C, D]), sb("res1", [P, C, D]), norm[2], norm[3]]
        stats = [sb(f"stats{n}", [P, C, 6]) for n in range(4)]
        meanvar = [sb(f"meanvar{n}", [P, C, 2]) for n in range(4)]
        vareps = [sb(f"vareps{n}", [P, C]) for n in range(4)]
        rstd = [sb(f"rstd{n}", [P, C]) for n in range(4)]
        hT, hT_full = zip(*(staged_pair(f"hT{n}", f"hT{n}_full", [P, C, N]) for n in range(3)))
        hid, hid_full = staged_pair("hid", "hid_full", [P, UC, N])
        adj1_in = sb("adj1_in", [P, C, N], i32)
        ao = pair("ao", [P, C, N])
        v_sb = sb("v_sb", [P, C, R * D])
        adj_top, adj_reaches = sb("adj_top", [P, 1]), sb("adj_reaches", [P, 1])
        adj_any, more_flag = sb("adj_any", [P, 1]), sb("more_flag", [P, 1], i32)
        s_max, s_nmax = sb("s_max", [P, 2 * HG * C]), sb("s_nmax", [P, 2 * HG * C])
        s_sum, s_rec = sb("s_sum", [P, 2 * HG * C]), sb("s_rec", [P, 2 * HG * C])

        ps_g = ps("ps_g", [P, 2, 512])
        ps_f = ps("ps_f", [P, 1, 512])
        ps_ao = ps("ps_ao", [P, 1, 512])
        ps1 = ps("ps1", [P, 4, 512])

        prep_a = event("prep_a", 0)
        prep_v = event("prep_v", 0)
        prep_p = event("prep_p", 0)
        gate_v = event("gate_v", 0)
        xT_loaded, x_loaded = event("xT_loaded", 16), event("x_loaded", 16)
        adj0_loaded, adj1_loaded = event("adj0_loaded", 16), event("adj1_loaded", 16)
        x_hi, x_lo = event("x_hi", 1), event("x_lo", 1)
        fence_set = event("fence_set", 1)
        wh_done = event("wh_done", 4)
        wh2_set = event("wh2_set", 2)
        pre_set = event("pre_set", 4)
        score_set = event("score_set", 2)
        g_max_set = event("g_max_set", 4)
        g_nmax_set = event("g_nmax_set", 2)
        att_set = event("att_set", 4)
        g_rec_set = event("g_rec_set", 2)
        whs_hi, whs_lo = event("whs_hi", 4), event("whs_lo", 4)
        att_hi, att_lo = event("att_hi", 2), event("att_lo", 2)
        mix_done = event("mix_done", 2)
        h1_hi, h1_lo = event("h1_hi", 1), event("h1_lo", 1)
        ysum = [event(f"ysum{n}", 1) for n in range(4)]
        stat_set = [event(f"stat_set{n}", 2) for n in range(4)]
        mv_set = [event(f"mv_set{n}", 2) for n in range(4)]
        ve_set = [event(f"ve_set{n}", 1) for n in range(4)]
        rstd_set = [event(f"rstd_set{n}", 1) for n in range(4)]
        norm_set = [event(f"norm_set{n}", 2) for n in range(4)]
        res_set = [event(f"res_set{n}", 2) for n in range(4)]
        turned = [event(f"turned{n}", 1) for n in range(3)]
        hT_set = [event(f"hT_set{n}", 2) for n in range(3)]
        hT_hi = [event(f"hT_hi{n}", 1) for n in range(3)]
        hT_lo = [event(f"hT_lo{n}", 1) for n in range(3)]
        up_done = [event(f"up_done{l}", UC // 2) for l in range(2)]
        hid_set = [event(f"hid_set{l}", UC) for l in range(2)]
        hid_hi = [event(f"hid_hi{l}", UC // 2) for l in range(2)]
        hid_lo = [event(f"hid_lo{l}", UC // 2) for l in range(2)]
        down_done = [event(f"down_done{l}", 1) for l in range(2)]
        adj_top_set, adj_reaches_set = event("adj_top_set", 1), event("adj_reaches_set", 1)
        adj_any_set, flag_set = event("adj_any_set", 1), event("flag_set", 1)
        gate_p, gate_t = event("gate_p", 0), event("gate_t", 0)
        qk_done, qk_set = event("qk_done", 2), event("qk_set", 4)
        v_done, v_set = event("v_done", 2), event("v_set", 2)
        v_more_done, v_more_set = event("v_more_done", 2), event("v_more_set", 2)
        s_done = event("s_done", HG)
        s_max_set, s_nmax_set = event("s_max_set", 4), event("s_nmax_set", 4)
        prob_set = event("prob_set", 4 * HG)
        s_rec_set = event("s_rec_set", 4)
        prob_scaled = event("prob_scaled", 4)
        prob_turned = event("prob_turned", 2 * HG)
        probT_set = event("probT_set", 2 * HG)
        masked_set, masked_more_set = event("masked_set", 4 * RA), event("masked_more_set", 4 * (R - RA))
        av_done, av_more_done = event("av_done", 2 * RA), event("av_more_done", 2 * (R - RA))
        ao_hi, ao_lo = event("ao_hi", 2), event("ao_lo", 2)
        wo_done = event("wo_done", 1)
        stored = event("stored", 16)

        def sp_features(sp, g):
            if not isinstance(g, int) or g > 0:
                sp.wait_ge(*wh_done(g - 1, 4))
            sp.dma_start(xT_in[:], xT[g].rearrange("(k p) n -> p k n", p=P)).then_inc(xT_loaded.sem, 16)

        def sp_edges0(sp, g):
            if not isinstance(g, int) or g > 0:
                sp.wait_ge(*g_max_set(g - 1, 4))
            sp.dma_start(adj0_in[:], adjT[g].rearrange("(k p) n -> p k n", p=P)).then_inc(adj0_loaded.sem, 16)

        def sp_nodes(sp, g):
            if not isinstance(g, int) or g > 0:
                sp.wait_ge(*turned[0](g - 1, 1))
                sp.wait_ge(*res_set[0](g - 1, 1))
            sp.dma_start(norm[0][:], x[g].rearrange("(k p) n -> p k n", p=P)).then_inc(x_loaded.sem, 16)

        def sp_edges1(sp, g):
            if not isinstance(g, int) or g > 0:
                sp.wait_ge(*masked_set(g - 1, 4 * RA))
                sp.wait_ge(*masked_more_set(g - 1, 4 * (R - RA)))
            sp.dma_start(adj1_in[:], adjT[g].rearrange("(k p) n -> p k n", p=P)).then_inc(adj1_loaded.sem, 16)

        def sp_store(sp, g):
            sp.wait_ge(*res_set[3](g, 2))
            sp.dma_start(out[g].rearrange("(k p) n -> p k n", p=P), norm[3][:]).then_inc(stored.sem, 16)

        def sp_body(sp, t, gat, att1, ff1):
            if gat:
                sp_features(sp, t + 3)
                sp_edges0(sp, t + 3)
                sp_nodes(sp, t + 3)
            if att1:
                sp_edges1(sp, t + 1)
            if ff1:
                sp_store(sp, t - 1)

        def product(ps_out, left, right, first, last):
            nc.tensor.matmul(ps_out, left[0], right[0], start=first, stop=False)
            nc.tensor.matmul(ps_out, left[0], right[1], start=False, stop=False)
            return nc.tensor.matmul(ps_out, left[1], right[0], start=False, stop=last)

        more = {}

        def cut(halves, *index):
            return tuple(h[(slice(None), *index)] for h in halves)

        def nodes(c):
            return slice(c * P, (c + 1) * P)

        WH1 = slice(N, 2 * N)

        def pe_gat_rows(pe, g, l):
            if l == 0:
                pe.wait_ge(*x_hi(g, 1))
                pe.wait_ge(*x_lo(g, 1))
                if not isinstance(g, int) or g > 0:
                    pe.wait_ge(*hT_set[0](g - 1, 2))
            else:
                pe.wait_ge(*h1_hi(g, 1))
                pe.wait_ge(*h1_lo(g, 1))
            for k in range(C):
                product(ps_g[:, 0, 0:D], cut(gT, k, nodes(0)), cut(gat_w[l], k, slice(0, D)), k == 0, k == C - 1)
            for k in range(C):
                last = product(ps_g[:, 0, WH1], cut(gat_a[l], k), cut(gT, k), k == 0, k == C - 1)
            last.then_inc(wh_done.sem, 1)

        def pe_gat_cols(pe, g, l):
            for k in range(C):
                product(ps_g[:, 1, 0:WE], cut(gT, k, nodes(1)), cut(gat_w[l], k), k == 0, k == C - 1)
            for k in range(C):
                for n, half in enumerate(cut(gT, k, nodes(0))):
                    last = nc.tensor.matmul(ps_g[:, 1, WE:WE + 2], half, gat_w[l][0][:, k, D:WE],
                                            start=(k == 0 and n == 0), stop=(k == C - 1 and n == 1))
            last.then_inc(wh_done.sem, 1)

        def pe_gat_mix(pe, g, l):
            pe.wait_ge(*whs_lo(g, 2 * l + 2))
            pe.wait_ge(*att_lo(g, l + 1))
            left, right = (wh_s, att_s) if l == 0 else (att_s, wh_s)
            for i in range(C):
                for k in range(C):
                    last = product(ps_g[:, 0, i * 256:(i + 1) * 256], cut(left, k, nodes(i)), cut(right, k),
                                   k == 0, k == C - 1)
            last.then_inc(mix_done.sem, 1)

        def pe_turn(pe, g, n, bank):
            pe.wait_ge(*norm_set[n](g, 2))
            for i in range(C):
                for f in range(C):
                    last = nc.tensor.transpose(bank[:, f * N + i * P:f * N + (i + 1) * P],
                                               norm[n][:, i, nodes(f)], ident[:])
            last.then_inc(turned[n].sem, 1)

        ff_in = [0, 2]

        def pe_up(pe, g, l, m):
            if m == 0:
                pe.wait_ge(*hT_hi[ff_in[l]](g, 1))
                pe.wait_ge(*hT_lo[ff_in[l]](g, 1))
                if l == 1 and (not isinstance(g, int) or g < B - 2):
                    pe.wait_ge(*hT_set[1](g + 2, 2))
                elif l == 1 and g > 0:
                    pe.wait_ge(*ysum[3](g - 1, 1))
                if l == 0 and (not isinstance(g, int) or g > 2):
                    pe.wait_ge(*ysum[3](g - 3, 1))
            else:
                pe.wait_ge(*hid_set[l](g, 2 * m))
            for u in range(2):
                for k in range(C):
                    last = product(ps_f[:, 0, u * N:(u + 1) * N], cut(up_w[l], k, nodes(2 * m + u)),
                                   cut(hT[ff_in[l]], k), k == 0, k == C - 1)
            last.then_inc(up_done[l].sem, 1)

        def pe_down(pe, g, l, i, half):
            if i == 0 and half == 0:
                pe.wait_ge(*hid_set[l](g, UC))
            for k in range(half * UC // 2, (half + 1) * UC // 2):
                if i == 0 and k % 2 == 0:
                    pe.wait_ge(*hid_lo[l](g, k // 2 + 1))
                last = product(ps_f[:, 0, i * D:(i + 1) * D], cut(hid, k, nodes(i)), cut(down_w[l], k),
                               k == 0, k == UC - 1)
            if i == C - 1 and half == 1:
                last.then_inc(down_done[l].sem, 1)

        def pe_qk(pe, g):
            pe.wait_ge(*hT_hi[1](g, 1))
            pe.wait_ge(*hT_lo[1](g, 1))
            if not isinstance(g, int) or g > 0:
                pe.wait_ge(*probT_set(g - 1, HG + 2))
            for b, w in enumerate((q_w, k_w)):
                for c in range(C):
                    for k in range(C):
                        last = product(ps1[:, b, c * N:(c + 1) * N], cut(w, k, nodes(c)), cut(hT[1], k),
                                       k == 0, k == C - 1)
                last.then_inc(qk_done.sem, 1)

        V_PARTS = [(0, 0), (1, 0), (0, 1), (1, 1)]

        def v_product(g, n):
            j, rr = V_PARTS[n]
            for k in range(C):
                last = product(ps_ao[:, 0, :], cut(hT[1], k, nodes(j)), cut(v_w, k, slice(rr * 512, rr * 512 + 512)),
                               k == 0, k == C - 1)
            return last

        def pe_v(pe, g, n):
            if n == 0 and (not isinstance(g, int) or g > 0):
                pe.wait_ge(*hT_set[2](g - 1, 2))
            if n:
                pe.wait_ge(*v_set(g, n))
            v_product(g, n).then_inc(v_done.sem, 1)

        def pe_flag(pe, g):
            pe.wait_ge(*flag_set(g, 1))
            pe.sem_inc(gate_t.sem, 1)
            more["pe"] = pe.value_load(more_flag[0:1, 0:1])

        def pe_v_more(pe, g):
            with pe.If(more["pe"] > 0):
                for n in range(2):
                    pe.wait_ge(*(v_more_set(g, 1) if n else v_set(g, 2)))
                    v_product(g, 2 + n).then_inc(v_more_done.sem, 1)
            with pe.Else():
                pe.sem_inc(v_more_done.sem, 2)

        def pe_scores(pe, g, hg, m):
            heads = (2 * m, 2 * m + 1)
            for h in heads:
                if hg == 0 and h == 0:
                    pe.wait_ge(*qk_set(g, 4))
                if hg == 0 and h >= 2 and (not isinstance(g, int) or g > 0):
                    pe.wait_ge(*probT_set(g - 1, HG + h + 1))
                if hg == 1:
                    pe.wait_ge(*probT_set(g, h + 1))
            for i in range(C):
                for h in heads:
                    rows = slice(h * DH, (h + 1) * DH)
                    last = nc.tensor.matmul(ps1[:, h, i * N:(i + 1) * N], qk[rows, 0, hg, nodes(i)],
                                            qk[rows, 1, hg, :], start=True, stop=True)
            last.then_inc(s_done.sem, 1)

        def pe_prob_turn(pe, g, hg, m):
            for h in (2 * m, 2 * m + 1):
                if h % 2 == 0:
                    pe.wait_ge(*prob_scaled(g, 2 * hg + h // 2 + 1))
                for i in range(C):
                    for j in range(C):
                        last = nc.tensor.transpose(ps1[:, h, j * N + i * P:j * N + (i + 1) * P],
                                                   prob[hg][:, h, i, nodes(j)], ident[:])
                last.then_inc(prob_turned.sem, 1)

        def av_product(hg, r):
            for j in range(C):
                for h in range(HG):
                    col = r * D + hg * P + h * DH
                    last = nc.tensor.matmul(ps_ao[h * DH:(h + 1) * DH, 0, hg * N:(hg + 1) * N],
                                            v_sb[:, j, col:col + DH],
                                            masked[:, r % 2, h, j * N:(j + 1) * N],
                                            start=(r == 0 and j == 0), stop=(r % RA == RA - 1 and j == C - 1),
                                            skip_group_check=True)
            return last

        def pe_av(pe, g, hg, r):
            if r == 0 and hg == 0:
                pe.wait_ge(*v_set(g, 2))
                pe.wait_ge(*v_more_set(g, 2))
            if r == 0 and hg == 1:
                pe.wait_ge(*ao_lo(g, 1))
            pe.wait_ge(*masked_set(g, 2 * (hg * RA + r) + 2))
            av_product(hg, r).then_inc(av_done.sem, 1)

        def pe_av_more(pe, g, hg):
            with pe.If(more["pe"] > 0):
                for r in range(RA, R):
                    pe.wait_ge(*masked_more_set(g, 2 * (hg * (R - RA) + r - RA) + 2))
                    av_product(hg, r).then_inc(av_more_done.sem, 1)
            with pe.Else():
                pe.sem_inc(av_more_done.sem, R - RA)

        def pe_wo(pe, g):
            pe.wait_ge(*ao_lo(g, 2))
            for i in range(C):
                for k in range(C):
                    last = product(ps_ao[:, 0, i * D:(i + 1) * D], cut(ao, k, nodes(i)), cut(o_w, k), k == 0, k == C - 1)
            last.then_inc(wo_done.sem, 1)

        def pe_body(pe, t, gat, ff0, att1, ff1):
            a, b, c, d = t + 1, t, t + 2, t - 1
            if att1:
                pe_qk(pe, b)
            if ff0:
                pe_up(pe, a, 0, 0)
            if att1:
                pe_scores(pe, b, 0, 0)
            if ff1:
                pe_wo(pe, d)
            if ff0:
                pe_up(pe, a, 0, 1)
            if att1:
                pe_scores(pe, b, 0, 1)
            if ff0:
                pe_up(pe, a, 0, 2)
            if gat:
                pe_gat_rows(pe, c, 0)
                pe_gat_cols(pe, c, 0)
            if att1:
                pe_prob_turn(pe, b, 0, 0)
            if ff0:
                pe_up(pe, a, 0, 3)
            if ff1:
                pe_turn(pe, d, 2, ps_ao[:, 0, :])
            if att1:
                pe_prob_turn(pe, b, 0, 1)
                pe_scores(pe, b, 1, 0)
                pe_scores(pe, b, 1, 1)
            if ff0:
                pe_down(pe, a, 0, 0, 0)
            if att1:
                pe_v(pe, b, 0)
            if gat:
                pe_gat_mix(pe, c, 0)
            if ff0:
                pe_down(pe, a, 0, 0, 1)
                pe_down(pe, a, 0, 1, 0)
                pe_down(pe, a, 0, 1, 1)
            if gat:
                pe_gat_rows(pe, c, 1)
                pe_gat_cols(pe, c, 1)
            if att1:
                pe_v(pe, b, 1)
                pe_prob_turn(pe, b, 1, 0)
                pe_flag(pe, b)
                pe_v_more(pe, b)
            if ff0:
                pe_turn(pe, a, 1, ps_f[:, 0, :])
            if att1:
                pe_av(pe, b, 0, 0)
            if ff1:
                pe_up(pe, d, 1, 0)
            if att1:
                pe_prob_turn(pe, b, 1, 1)
                pe_av(pe, b, 0, 1)
                pe_av_more(pe, b, 0)
            if ff1:
                pe_up(pe, d, 1, 1)
            if gat:
                pe_gat_mix(pe, c, 1)
            if ff1:
                pe_up(pe, d, 1, 2)
            if att1:
                pe_av(pe, b, 1, 0)
            if ff1:
                pe_up(pe, d, 1, 3)
            if att1:
                pe_av(pe, b, 1, 1)
            if ff1:
                pe_down(pe, d, 1, 0, 0)
            if att1:
                pe_av_more(pe, b, 1)
            if ff1:
                pe_down(pe, d, 1, 0, 1)
                pe_down(pe, d, 1, 1, 0)
            if gat:
                pe_turn(pe, c, 0, ps_g[:, 1, :])
            if ff1:
                pe_down(pe, d, 1, 1, 1)

        def act_gat_pre(act, g, l):
            act.wait_ge(*wh_done(g, 2 * l + 1))
            act.wait_ge(*wh2_set(g, l + 1))
            for j in range(C):
                act.activation(score[:, j, :], ps_g[:, 0, WH1], ACT.Identity, bias=wh2[:, 1 - j:2 - j]).then_inc(pre_set.sem, 1)

        def act_gat_exp(act, g, l):
            act.wait_ge(*g_nmax_set(g, l + 1))
            for j in range(C):
                act.activation(score[:, j, :], score[:, j, :], ACT.Exp, bias=g_nmax[:, j:j + 1],
                               accum_out=g_sum[:, j:j + 1]).then_inc(att_set.sem, 1)

        def act_h1(act, g):
            act.wait_ge(*mix_done(g, 1))
            act.activation(gT[0][:].rearrange("p c n -> p (c n)"), ps_g[:, 0, :], ACT.Copy).then_inc(h1_hi.sem, 1)

        def act_turned(act, g, n, bank):
            act.wait_ge(*turned[n](g, 1))
            for f in range(C):
                act.activation(hT_full[n][:, f, :], bank[:, f * N:(f + 1) * N], ACT.Identity,
                               bias=shift_col[n][:, f:f + 1], scale=gain_col[n][:, f:f + 1]).then_inc(hT_set[n].sem, 1)
            act.wait_ge(*hT_set[n](g, 2))
            act.activation(hT[n][0][:], hT_full[n][:], ACT.Copy).then_inc(hT_hi[n].sem, 1)

        def act_hidden(act, g, l, m):
            act.wait_ge(*up_done[l](g, m + 1))
            for u in range(2):
                act.activation(hid_full[:, 2 * m + u, :], ps_f[:, 0, u * N:(u + 1) * N],
                               ACT.Relu if l == 0 else ACT.Gelu,
                               bias=up_bias[l][:, 2 * m + u:2 * m + u + 1]).then_inc(hid_set[l].sem, 1)
            act.wait_ge(*hid_set[l](g, 2 * m + 2))
            act.activation(hid[0][:, 2 * m:2 * m + 2, :], hid_full[:, 2 * m:2 * m + 2, :], ACT.Copy).then_inc(hid_hi[l].sem, 1)

        def act_qk(act, g):
            for b in range(2):
                act.wait_ge(*qk_done(g, b + 1))
                for c in range(C):
                    act.activation(qk[:, b, c, :], ps1[:, b, c * N:(c + 1) * N], ACT.Identity,
                                   bias=qk_bias[:, b, c:c + 1]).then_inc(qk_set.sem, 1)

        def act_prob(act, g, hg, m):
            for h in (2 * m, 2 * m + 1):
                if h % 2 == 0:
                    act.wait_ge(*s_nmax_set(g, 2 * hg + h // 2 + 1))
                for i in range(C):
                    col = (hg * HG + h) * C + i
                    act.activation(prob[hg][:, h, i, :], ps1[:, h, i * N:(i + 1) * N], ACT.Exp,
                                   bias=s_nmax[:, col:col + 1], scale=SCALE,
                                   accum_out=s_sum[:, col:col + 1]).then_inc(prob_set.sem, 1)

        def act_prob_turned(act, g, hg, m):
            for h in (2 * m, 2 * m + 1):
                act.wait_ge(*prob_turned(g, hg * HG + h + 1))
                act.activation(prob[hg][:, h, :, :].rearrange("p c n -> p (c n)"), ps1[:, h, :],
                               ACT.Copy).then_inc(probT_set.sem, 1)

        def act_ao(act, g, hg):
            act.wait_ge(*av_done(g, (hg + 1) * RA))
            act.wait_ge(*av_more_done(g, (hg + 1) * (R - RA)))
            act.activation(ao[0][:, hg, :], ps_ao[:, 0, hg * N:(hg + 1) * N], ACT.Copy).then_inc(ao_hi.sem, 1)

        def act_body(act, t, gat, ff0, att1, ff1):
            a, b, c, d = t + 1, t, t + 2, t - 1
            if att1:
                act_qk(act, b)
            if ff0:
                act_hidden(act, a, 0, 0)
            if att1:
                act_prob(act, b, 0, 0)
            if ff0:
                act_hidden(act, a, 0, 1)
            if att1:
                act_prob(act, b, 0, 1)
            if ff0:
                act_hidden(act, a, 0, 2)
            if gat:
                act_gat_pre(act, c, 0)
            if att1:
                act_prob_turned(act, b, 0, 0)
                act_prob_turned(act, b, 0, 1)
            if ff0:
                act_hidden(act, a, 0, 3)
            if gat:
                act_gat_exp(act, c, 0)
            if ff1:
                act_turned(act, d, 2, ps_ao[:, 0, :])
            if att1:
                act_prob(act, b, 1, 0)
            if gat:
                act_h1(act, c)
            if att1:
                act_prob(act, b, 1, 1)
            if gat:
                act_gat_pre(act, c, 1)
            if att1:
                act_prob_turned(act, b, 1, 0)
            if ff0:
                act_turned(act, a, 1, ps_f[:, 0, :])
            if gat:
                act_gat_exp(act, c, 1)
            if ff1:
                act_hidden(act, d, 1, 0)
            if att1:
                act_prob_turned(act, b, 1, 1)
                act_ao(act, b, 0)
            if ff1:
                act_hidden(act, d, 1, 1)
                act_hidden(act, d, 1, 2)
                act_hidden(act, d, 1, 3)
            if gat:
                act_turned(act, c, 0, ps_g[:, 1, :])
            if att1:
                act_ao(act, b, 1)

        def dve_gat_in(dve, g):
            dve.wait_ge(*xT_loaded(g, 16))
            dve.tensor_copy(gT[0][:], xT_in[:]).then_inc(x_hi.sem, 1)

        def dve_fence(dve, g):
            dve.wait_ge(*adj0_loaded(g, 16))
            dve.tensor_scalar(fence, adj0_in[:], 0.0, NEG, ALU.is_le, ALU.mult).then_inc(fence_set.sem, 1)

        def dve_gat_wh2(dve, g, l):
            dve.wait_ge(*wh_done(g, 2 * l + 2))
            dve.tensor_reduce(wh2[:], ps_g[:, 1, D:D + 4].rearrange("p (j h) -> p j h", h=2), AX.X,
                              ALU.add).then_inc(wh2_set.sem, 1)

        def dve_gat_score(dve, g, l):
            dve.wait_ge(*pre_set(g, 2 * l + 2))
            dve.scalar_tensor_tensor(out=score[:], in0=score[:], scalar=ALPHA, in1=score[:],
                                     op0=ALU.mult, op1=ALU.max).then_inc(score_set.sem, 1)
            dve.wait_ge(*score_set(g, l + 1))
            if l == 0:
                dve.wait_ge(*fence_set(g, 1))
            dve.sem_inc(gate_v.sem, 1)
            for j in range(C):
                dve.tensor_tensor_reduce(out=score[:, j, :], in0=score[:, j, :], in1=fence[:, j, :], scale=1.0,
                                         scalar=-3.0e38, op0=ALU.add, op1=ALU.max,
                                         accum_out=g_max[:, j:j + 1]).then_inc(g_max_set.sem, 1)
            dve.wait_ge(*g_max_set(g, 2 * l + 2))
            dve.tensor_scalar(g_nmax[:], g_max[:], -1.0, None, ALU.mult).then_inc(g_nmax_set.sem, 1)

        def dve_gat_split(dve, g, l):
            dve.wait_ge(*att_set(g, 2 * l + 2))
            dve.reciprocal(g_rec[:], g_sum[:]).then_inc(g_rec_set.sem, 1)
            dve.tensor_copy(att_s[0][:], score[:]).then_inc(att_hi.sem, 1)
            dve.wait_ge(*g_rec_set(g, l + 1))
            for j in range(C):
                dve.tensor_scalar(wh_s[0][:, j, :], ps_g[:, j, 0:D], g_rec[:, j:j + 1], None,
                                  ALU.mult).then_inc(whs_hi.sem, 1)
            dve.wait_ge(*att_hi(g, l + 1))
            dve.tensor_tensor(att_s[1][:], score[:], value(att_s[0][:]), ALU.subtract).then_inc(att_lo.sem, 1)
            dve.wait_ge(*whs_hi(g, 2 * l + 2))
            for j in range(C):
                dve.scalar_tensor_tensor(out=wh_s[1][:, j, :], in0=ps_g[:, j, 0:D], scalar=g_rec[:, j:j + 1],
                                         in1=value(wh_s[0][:, j, :]), op0=ALU.mult,
                                         op1=ALU.subtract).then_inc(whs_lo.sem, 1)

        def dve_h1(dve, g):
            dve.wait_ge(*h1_hi(g, 1))
            dve.tensor_tensor(gT[1][:].rearrange("p c n -> p (c n)"), ps_g[:, 0, :],
                              value(gT[0][:]).rearrange("p c n -> p (c n)"), ALU.subtract).then_inc(h1_lo.sem, 1)

        ln_bank = [ps_g[:, 0, :], ps_f[:, 0, :], ps_ao[:, 0, :], ps_f[:, 0, :]]
        ln_done = [lambda g: mix_done(g, 2), lambda g: down_done[0](g, 1), lambda g: wo_done(g, 1),
                   lambda g: down_done[1](g, 1)]

        def dve_norm(dve, g, n):
            dve.wait_ge(*ln_done[n](g))
            dve.wait_ge(*(x_loaded(g, 16) if n == 0 else res_set[n - 1](g, 2)))
            if n == 1 and (not isinstance(g, int) or g > 0):
                dve.wait_ge(*res_set[1](g - 1, 1))
            if n == 3 and (not isinstance(g, int) or g > 0):
                dve.wait_ge(*stored(g - 1, 16))
            residual = norm[0] if n == 0 else res[n - 1]
            y = norm[n]
            dve.tensor_tensor(y[:].rearrange("p c n -> p (c n)"), ln_bank[n],
                              residual[:].rearrange("p c n -> p (c n)"), ALU.add).then_inc(ysum[n].sem, 1)
            dve.wait_ge(*ysum[n](g, 1))
            for i in range(C):
                dve.bn_stats(stats[n][:, i, :], y[:, i, :]).then_inc(stat_set[n].sem, 1)
            dve.wait_ge(*stat_set[n](g, 2))
            dve.sem_inc(gate_v.sem, 1)
            for i in range(C):
                dve.bn_aggr(meanvar[n][:, i, :], stats[n][:, i, :]).then_inc(mv_set[n].sem, 1)
            dve.wait_ge(*mv_set[n](g, 2))
            dve.tensor_scalar(vareps[n][:].unsqueeze(2), meanvar[n][:, :, 1:2], EPS, None, ALU.add).then_inc(ve_set[n].sem, 1)

        def dve_norm_end(dve, g, n):
            dve.wait_ge(*rstd_set[n](g, 1))
            for i in range(C):
                dve.tensor_scalar(norm[n][:, i, :], norm[n][:, i, :], meanvar[n][:, i, 0:1], rstd[n][:, i:i + 1],
                                  ALU.subtract, ALU.mult).then_inc(norm_set[n].sem, 1)

        def dve_adj_top(dve, g):
            dve.wait_ge(*adj1_loaded(g, 16))
            dve.tensor_reduce(adj_top[:], adj1_in[:], AX.XY, ALU.max).then_inc(adj_top_set.sem, 1)
            dve.wait_ge(*adj_top_set(g, 1))
            dve.tensor_scalar(adj_reaches[:], adj_top[:], float(RA), None, ALU.is_ge).then_inc(adj_reaches_set.sem, 1)

        def dve_flag(dve, g):
            dve.wait_ge(*flag_set(g, 1))
            dve.sem_inc(gate_v.sem, 1)
            more["dve"] = dve.value_load(more_flag[0:1, 0:1])

        def v_out(n):
            j, rr = V_PARTS[n]
            return nc.vector.tensor_tensor(v_sb[:, j, rr * 512:(rr + 1) * 512], ps_ao[:, 0, :],
                                           v_bias[:, rr * 512:(rr + 1) * 512], ALU.add)

        def dve_v(dve, g, n):
            dve.wait_ge(*v_done(g, n + 1))
            v_out(n).then_inc(v_set.sem, 1)

        def dve_v_more(dve, g):
            with dve.If(more["dve"] > 0):
                for n in range(2):
                    dve.wait_ge(*v_more_done(g, n + 1))
                    v_out(2 + n).then_inc(v_more_set.sem, 1)
            with dve.Else():
                dve.sem_inc(v_more_set.sem, 2)

        def dve_max(dve, g, hg, m):
            cols = slice((hg * HG + 2 * m) * C, (hg * HG + 2 * m + 2) * C)
            k = 2 * hg + m + 1
            dve.wait_ge(*s_done(g, k))
            dve.tensor_reduce(s_max[:, cols], ps1[:, 2 * m:2 * m + 2, :].rearrange("p b (c n) -> p (b c) n", n=N),
                              AX.X, ALU.max).then_inc(s_max_set.sem, 1)
            dve.wait_ge(*s_max_set(g, k))
            dve.tensor_scalar(s_nmax[:, cols], s_max[:, cols], -SCALE, None, ALU.mult).then_inc(s_nmax_set.sem, 1)

        def dve_rec(dve, g, hg, m):
            cols = slice((hg * HG + 2 * m) * C, (hg * HG + 2 * m + 2) * C)
            dve.wait_ge(*prob_set(g, C * (hg * HG + 2 * m + 2)))
            dve.reciprocal(s_rec[:, cols], s_sum[:, cols]).then_inc(s_rec_set.sem, 1)

        def mask_pair(hg, r, m):
            return nc.vector.scalar_tensor_tensor(
                out=masked[:, r % 2, 2 * m:2 * m + 2, :],
                in0=adj1_in[:].rearrange("p c n -> p (c n)").unsqueeze(1).broadcast_to([P, 2, C * N]), scalar=float(r),
                in1=prob[hg][:, 2 * m:2 * m + 2, :, :].rearrange("p h c n -> p h (c n)"),
                op0=ALU.is_equal, op1=ALU.mult)

        def dve_mask(dve, g, hg, r):
            if hg == 0 and r == 0:
                dve.wait_ge(*adj1_loaded(g, 16))
            if hg == 1:
                dve.wait_ge(*av_done(g, r + 1))
                dve.wait_ge(*av_more_done(g, r + 1))
            for m in range(2):
                if r == 0:
                    dve.wait_ge(*probT_set(g, hg * HG + 2 * m + 2))
                mask_pair(hg, r, m).then_inc(masked_set.sem, 1)

        def dve_mask_more(dve, g, hg):
            with dve.If(more["dve"] > 0):
                for r in range(RA, R):
                    dve.wait_ge(*av_done(g, hg * RA + r - RA + 1))
                    for m in range(2):
                        mask_pair(hg, r, m).then_inc(masked_more_set.sem, 1)
            with dve.Else():
                dve.sem_inc(masked_more_set.sem, 2 * (R - RA))

        def dve_ao(dve, g, hg):
            dve.wait_ge(*ao_hi(g, hg + 1))
            dve.tensor_tensor(ao[1][:, hg, :], ps_ao[:, 0, hg * N:(hg + 1) * N], value(ao[0][:, hg, :]),
                              ALU.subtract).then_inc(ao_lo.sem, 1)

        def dve_body(dve, t, gat, ff0, att1, ff1):
            a, b, c, d = t + 1, t, t + 2, t - 1
            if gat:
                dve_gat_in(dve, c)
            if att1:
                dve_adj_top(dve, b)
                dve_max(dve, b, 0, 0)
            if ff1:
                dve_norm(dve, d, 2)
            if gat:
                dve_fence(dve, c)
            if att1:
                dve_rec(dve, b, 0, 0)
                dve_max(dve, b, 0, 1)
                dve_rec(dve, b, 0, 1)
            if gat:
                dve_gat_wh2(dve, c, 0)
            if ff1:
                dve_norm_end(dve, d, 2)
            if gat:
                dve_gat_score(dve, c, 0)
            if att1:
                dve_mask(dve, b, 0, 0)
            if gat:
                dve_gat_split(dve, c, 0)
            if att1:
                dve_max(dve, b, 1, 0)
                dve_mask(dve, b, 0, 1)
                dve_rec(dve, b, 1, 0)
                dve_v(dve, b, 0)
            if gat:
                dve_h1(dve, c)
            if att1:
                dve_max(dve, b, 1, 1)
            if ff0:
                dve_norm(dve, a, 1)
            if att1:
                dve_rec(dve, b, 1, 1)
            if gat:
                dve_gat_wh2(dve, c, 1)
            if ff0:
                dve_norm_end(dve, a, 1)
            if att1:
                dve_v(dve, b, 1)
                dve_flag(dve, b)
                dve_v_more(dve, b)
            if gat:
                dve_gat_score(dve, c, 1)
            if att1:
                dve_mask_more(dve, b, 0)
            if gat:
                dve_gat_split(dve, c, 1)
            if att1:
                dve_mask(dve, b, 1, 0)
                dve_ao(dve, b, 0)
                dve_mask(dve, b, 1, 1)
            if gat:
                dve_norm(dve, c, 0)
                dve_norm_end(dve, c, 0)
            if att1:
                dve_mask_more(dve, b, 1)
            if ff1:
                dve_norm(dve, d, 3)
            if att1:
                dve_ao(dve, b, 1)
            if ff1:
                dve_norm_end(dve, d, 3)

        def pool_gat_in(pool, g):
            pool.wait_ge(*x_hi(g, 1))
            pool.tensor_tensor(gT[1][:], xT_in[:], value(gT[0][:]), ALU.subtract).then_inc(x_lo.sem, 1)

        def pool_rstd(pool, g, n):
            pool.wait_ge(*ve_set[n](g, 1))
            pool.tensor_tensor(rstd[n][:], vareps[n][:], neg_half[:], ALU.pow).then_inc(rstd_set[n].sem, 1)

        def pool_affine(pool, g, n):
            pool.wait_ge(*norm_set[n](g, 2))
            if n == 2:
                pool.wait_ge(*turned[n](g, 1))
            if n in (0, 1) and (not isinstance(g, int) or g > 0):
                pool.wait_ge(*ysum[n + 1](g - 1, 1))
            pool.tensor_tensor(res[n][:], norm[n][:], gain_row[n][:].unsqueeze(1).broadcast_to([P, C, D]),
                               ALU.mult).then_inc(res_set[n].sem, 1)
            pool.wait_ge(*res_set[n](g, 1))
            pool.tensor_tensor(res[n][:], res[n][:], shift_row[n][:].unsqueeze(1).broadcast_to([P, C, D]),
                               ALU.add).then_inc(res_set[n].sem, 1)

        def pool_hT(pool, g, n):
            pool.wait_ge(*hT_hi[n](g, 1))
            pool.tensor_tensor(hT[n][1][:], hT_full[n][:], value(hT[n][0][:]), ALU.subtract).then_inc(hT_lo[n].sem, 1)

        def pool_hidden(pool, g, l, m):
            pool.wait_ge(*hid_hi[l](g, m + 1))
            pool.tensor_tensor(hid[1][:, 2 * m:2 * m + 2, :], hid_full[:, 2 * m:2 * m + 2, :],
                               value(hid[0][:, 2 * m:2 * m + 2, :]), ALU.subtract).then_inc(hid_lo[l].sem, 1)

        def pool_prob(pool, g, hg, m):
            first = (hg * HG + 2 * m) * C
            pool.wait_ge(*s_rec_set(g, 2 * hg + m + 1))
            part = prob[hg][:, 2 * m:2 * m + 2, :, :].rearrange("p h c n -> p (h c) n")
            pool.tensor_tensor(part, part, s_rec[:, first:first + 2 * C].unsqueeze(2).broadcast_to([P, 2 * C, N]),
                               ALU.mult).then_inc(prob_scaled.sem, 1)

        def pool_flag(pool, g):
            pool.wait_ge(*adj_reaches_set(g, 1))
            pool.sem_inc(gate_p.sem, 1)
            pool.partition_all_reduce(adj_any[:], adj_reaches[:], P, bass.bass_isa.ReduceOp.max).then_inc(adj_any_set.sem, 1)
            pool.wait_ge(*adj_any_set(g, 1))
            pool.sem_inc(gate_p.sem, 1)
            pool.tensor_copy(more_flag[:], adj_any[:]).then_inc(flag_set.sem, 1)

        def pool_body(pool, t, gat, ff0, att1, ff1):
            a, b, c, d = t + 1, t, t + 2, t - 1
            if gat:
                pool_gat_in(pool, c)
            if att1:
                pool_flag(pool, b)
            if ff0:
                pool_hidden(pool, a, 0, 0)
            if ff1:
                pool_rstd(pool, d, 2)
            if att1:
                pool_prob(pool, b, 0, 0)
            if ff0:
                pool_hidden(pool, a, 0, 1)
            if att1:
                pool_prob(pool, b, 0, 1)
            if ff0:
                pool_hidden(pool, a, 0, 2)
            if ff1:
                pool_hT(pool, d, 2)
            if ff0:
                pool_hidden(pool, a, 0, 3)
            if att1:
                pool_affine(pool, b, 1)
                pool_prob(pool, b, 1, 0)
            if ff0:
                pool_rstd(pool, a, 1)
            if att1:
                pool_prob(pool, b, 1, 1)
            if ff0:
                pool_hT(pool, a, 1)
            if ff1:
                pool_affine(pool, d, 2)
            if ff1:
                pool_hidden(pool, d, 1, 0)
                pool_hidden(pool, d, 1, 1)
                pool_hidden(pool, d, 1, 2)
                pool_hidden(pool, d, 1, 3)
            if gat:
                pool_rstd(pool, c, 0)
                pool_affine(pool, c, 0)
                pool_hT(pool, c, 0)
            if ff1:
                pool_rstd(pool, d, 3)
                pool_affine(pool, d, 3)

        def rows(w):
            return w.rearrange("(k p) n -> p k n", p=P)

        def across(v):
            return v.unsqueeze(0).broadcast_to([P, v.shape[0]])

        def columns(tile, v):
            return tile, v.rearrange("(c p) -> p c", p=P)

        gains = [p0["g_ln1"], p0["g_ln2"], p1["g1"], p1["g2"]]
        shifts = [p0["b_ln1"], p0["b_ln2"], p1["beta1"], p1["beta2"]]
        groups = [
            [(raw_gat[l][:, :, 0:D], rows(p0[f"W{l + 1}"])) for l in range(2)]
            + [(raw_a[l][:], across(p0[f"a{l + 1}"].rearrange("n o -> (n o)"))) for l in range(2)],
            [(raw_up[0][:], rows(p0["w_ff1"]))],
            [(raw_down[0][:], rows(p0["w_ff2"]))],
            [(raw_qko[m][:], rows(p1[w])) for m, w in enumerate(("Wq", "Wk", "Wo"))],
            [(raw_v[:, :, r * D:(r + 1) * D], rows(p1["Wv"][r])) for r in range(R)],
            [(raw_up[1][:], rows(p1["W1"]))],
            [(raw_down[1][:], rows(p1["W2"]))],
            [(gain_row[n][:], across(gains[n])) for n in range(4)]
            + [(shift_row[n][:], across(shifts[n])) for n in range(4)]
            + [(raw_next[n][:], across(v)) for n, v in enumerate((p0["b_ff2"], p1["bo"], p1["b2"]))]
            + [(v_bias[:, r * D:(r + 1) * D], across(p1["bv"][r])) for r in range(R)]
            + [columns(gain_col[n][:], gains[n]) for n in range(3)]
            + [columns(shift_col[n][:], shifts[n]) for n in range(3)]
            + [columns(up_bias[0][:], p0["b_ff1"]), columns(up_bias[1][:], p1["b1"])]
            + [columns(qk_bias[:, 0, :], p1["bq"]), columns(qk_bias[:, 1, :], p1["bk"])],
        ]
        params_in = [ctx.enter_context(nc.semaphore(f"params_in{n}")) for n in range(len(groups))]
        splits = [[(raw_up[0], up_w[0])], [(raw_down[0], down_w[0])],
                  [(raw_qko[0], q_w), (raw_qko[1], k_w), (raw_qko[2], o_w)], [(raw_v, v_w)],
                  [(raw_up[1], up_w[1])], [(raw_down[1], down_w[1])]]
        POOL_SPLITS = (1, 4)
        gat_splits = [(raw_gat[l], gat_w[l]) for l in range(2)] + [(raw_arep[l], gat_a[l]) for l in range(2)]
        WA, PLACED = 8, 8 + 6
        HI = PLACED + len(gat_splits)
        LO = HI + len(gat_splits)
        PREP_V = LO + 4 + sum(len(g) for n, g in enumerate(splits) if n not in POOL_SPLITS) + 3
        PREP_P = 4 + len(POOL_SPLITS)
        PREP_A = sum(len(g) for g in splits)

        def sp_setup(sp):
            for group, there in zip(groups, params_in):
                for dst, src in group:
                    sp.dma_start(dst, src, allow_slow_non_contiguous=True).then_inc(there, 16)
            ready(sp)

        def act_setup(act):
            for n, group in enumerate(splits):
                act.wait_ge(params_in[n + 1], 16 * len(groups[n + 1]))
                for raw, (hi, _) in group:
                    act.activation(hi[:], raw[:], ACT.Copy).then_inc(prep_a.sem, 1)

        def split_lo(eng, n, done):
            eng.wait_ge(prep_a.sem, sum(len(g) for g in splits[:n + 1]))
            for raw, (hi, lo) in splits[n]:
                eng.tensor_tensor(lo[:], raw[:], value(hi), ALU.subtract).then_inc(done.sem, 1)

        def dve_setup(dve):
            dve.wait_ge(params_in[0], 16 * len(groups[0]))
            for l in range(2):
                for half in range(2):
                    for k in range(C):
                        dst = raw_wa[:, l, k:k + 1] if half == 0 else raw_gat[l][:, k, D:D + 1]
                        dve.tensor_tensor_reduce(out=raw_prod[:, l, half, k, :], in0=raw_gat[l][:, k, 0:D],
                                                 in1=raw_a[l][:, half * D:(half + 1) * D], scale=1.0, scalar=0.0,
                                                 op0=ALU.mult, op1=ALU.add, accum_out=dst).then_inc(prep_v.sem, 1)
            for l in range(2):
                dve.memset(raw_gat[l][:, :, D + 1:WE], 0.0).then_inc(prep_v.sem, 1)
            dve.wait_ge(prep_v.sem, WA)
            for l in range(2):
                for k in range(C):
                    dve.tensor_copy(raw_arep[l][:, k, :], raw_wa[:, l, k:k + 1].broadcast_to([P, P])).then_inc(prep_v.sem, 1)
            dve.wait_ge(prep_v.sem, PLACED)
            for raw, (hi, _) in gat_splits:
                dve.tensor_copy(hi[:], raw[:]).then_inc(prep_v.sem, 1)
            dve.wait_ge(prep_v.sem, HI)
            for raw, (hi, lo) in gat_splits:
                dve.tensor_tensor(lo[:], raw[:], value(hi), ALU.subtract).then_inc(prep_v.sem, 1)
            dve.wait_ge(prep_v.sem, LO)
            for l in range(2):
                hi, lo = gat_w[l]
                dve.tensor_copy(hi[:, :, D + 1:WE], value(lo)[:, :, D:D + 1]).then_inc(prep_v.sem, 1)
            dve.wait_ge(prep_v.sem, LO + 2)
            for l in range(2):
                dve.tensor_copy(gat_w[l][1][:, :, D:WE],
                                raw_gat[l][:, :, D + 1:WE].broadcast_to([P, C, 2])).then_inc(prep_v.sem, 1)
            for n in range(len(splits)):
                if n not in POOL_SPLITS:
                    split_lo(dve, n, prep_v)
            dve.wait_ge(params_in[-1], 16 * len(groups[-1]))
            for n in range(3):
                dve.tensor_tensor(shift_row[n][:], shift_row[n][:], raw_next[n][:], ALU.add).then_inc(prep_v.sem, 1)
            ready(dve)

        def pool_setup(pool):
            pool.memset(ident[:], 0.0).then_inc(prep_p.sem, 1)
            pool.memset(neg_half[:], -0.5).then_inc(prep_p.sem, 1)
            pool.wait_ge(prep_p.sem, 2)
            pool.affine_select(out=ident[:], in_=ident[:], compare_op=ALU.not_equal, fill=1.0, base=0,
                               pattern=[[-1, P]], channel_multiplier=1).then_inc(prep_p.sem, 2)
            for n in POOL_SPLITS:
                split_lo(pool, n, prep_p)
            ready(pool)

        def ready(eng):
            eng.wait_ge(prep_a.sem, PREP_A)
            eng.wait_ge(prep_v.sem, PREP_V)
            eng.wait_ge(prep_p.sem, PREP_P)
            for group, there in zip(groups, params_in):
                eng.wait_ge(there, 16 * len(group))

        def run(eng, body):
            body(eng, -2, True, False, False, False)
            body(eng, -1, True, True, False, False)
            body(eng, 0, True, True, True, False)
            body(eng, 1, True, True, True, True)
            with eng.Fori(2, B - 2) as t:
                body(eng, t, True, True, True, True)
            body(eng, B - 2, False, True, True, True)
            body(eng, B - 1, False, False, True, True)
            body(eng, B, False, False, False, True)

        def sp_run(sp):
            sp_features(sp, 0)
            sp_edges0(sp, 0)
            sp_nodes(sp, 0)
            sp_edges1(sp, 0)
            sp_body(sp, -2, True, False, False)
            sp_body(sp, -1, True, False, False)
            sp_body(sp, 0, True, True, False)
            with sp.Fori(1, B - 3) as t:
                sp_body(sp, t, True, True, True)
            sp_body(sp, B - 3, False, True, True)
            sp_body(sp, B - 2, False, True, True)
            sp_body(sp, B - 1, False, False, True)
            sp_body(sp, B, False, False, True)

        block = ctx.enter_context(nc.Block())

        @block.sync
        def _(sp):
            sp_setup(sp)
            sp_run(sp)
            sp.wait_ge(*stored(B - 1, 16))

        @block.tensor
        def _(pe):
            ready(pe)
            run(pe, pe_body)

        @block.scalar
        def _(act):
            act_setup(act)
            ready(act)
            run(act, act_body)

        @block.vector
        def _(dve):
            dve_setup(dve)
            run(dve, dve_body)

        @block.gpsimd
        def _(pool):
            pool_setup(pool)
            run(pool, pool_body)


_L0 = ["W1", "a1", "W2", "a2", "w_ff1", "b_ff1", "w_ff2", "b_ff2", "g_ln1", "b_ln1", "g_ln2", "b_ln2"]
_L1 = ["Wq", "bq", "Wk", "bk", "Wv", "bv", "Wo", "bo", "W1", "b1", "W2", "b2", "g1", "beta1", "g2", "beta2"]


def kernel(**inputs):
    import numpy as np
    import concourse.bacc as bacc
    from concourse.bass_utils import run_bass_kernel_spmd

    nc = bacc.Bacc("TRN2", target_bir_lowering=False, num_devices=1, dynamic_dma_scratch_size=1024)
    arrays = {}

    def given(name, a):
        a = np.ascontiguousarray(a)
        arrays[name] = a
        return nc.dram_tensor(name, a.shape, mybir.dt.from_np(a.dtype), kind="ExternalInput").ap()

    xs, adj = np.asarray(inputs["x"]), np.asarray(inputs["adj"])
    x = given("x_nodes", xs)
    xT = given("x_features", xs.transpose(0, 2, 1))
    adjT = given("adj_keys", adj.transpose(0, 2, 1))
    p0 = {n: given(f"L0_{n}", inputs[f"L0_gnn_{n}"]) for n in _L0}
    p1 = {n: given(f"L1_{n}", inputs[f"L1_gnn_{n}"]) for n in _L1}
    out = nc.dram_tensor("out_nodes", xs.shape, mybir.dt.float32, kind="ExternalOutput").ap()
    adj_seq_kernel(nc, x, xT, adjT, p0, p1, out)
    r = run_bass_kernel_spmd(nc, [arrays], core_ids=[0])
    return r.results[0]["out_nodes"]
```
